# Optimizing a Trainium2 kernel written in Bass

```python
import numpy as np
import jax
import jax.numpy as jnp

def _softmax(x, axis=-1):
    return jax.nn.softmax(x, axis=axis)

def _gelu(x):
    return jax.nn.gelu(x, approximate=True)

def _silu(x):
    return jax.nn.silu(x)

def _sigmoid(x):
    return jax.nn.sigmoid(x)

def _layernorm(x, axis=-1, eps=1e-05):
    m = jnp.mean(x, axis=axis, keepdims=True)
    v = jnp.var(x, axis=axis, keepdims=True)
    return (x - m) / jnp.sqrt(v + eps)

def _scatter_add(tgt, idx, src, axis=0):
    return tgt.at[idx].add(src)

def _segment_sum(src, seg, n):
    return jax.ops.segment_sum(src, seg, n)
kernel_name = 'mk_xattn_seq_d2_seqx_r2_eb1a96'

def setup_inputs(seed: int=0):
    np.random.seed(seed)
    _w = jnp.asarray

    def _rec_inputs():
        import jax
        import jax.numpy as jnp
        _rk = jax.random.key(seed)
        x = 7.22e-05 + 1 * jax.random.normal(jax.random.fold_in(_rk, 1), (4, 1024, 1024), jnp.float32)
        _lenS = 1024 - jax.random.randint(jax.random.fold_in(_rk, 7), (4,), 0, max(1, 1024 // 4) + 1, jnp.int32)
        _lenS2 = 64 - jax.random.randint(jax.random.fold_in(_rk, 8), (4,), 0, max(1, 64 // 4) + 1, jnp.int32)
        _ctx_2048P = jax.random.normal(jax.random.fold_in(_rk, 11), (4, 16, 1024), jnp.float32)
        _ctx_2048c = jax.random.dirichlet(jax.random.fold_in(_rk, 511), 0.3 * jnp.ones((16,), jnp.float32), (4, 64))
        _ctx_2048t = jnp.einsum('bsk,bkd->bsd', _ctx_2048c, _ctx_2048P)
        _ctx_2048t = _ctx_2048t * jax.lax.rsqrt(jnp.mean(jnp.square(_ctx_2048t)) + 1e-12) * 0.953939
        ctx_2048 = 4.13588e-05 + 0.999923 * (_ctx_2048t + 0.3 * jax.random.normal(jax.random.fold_in(_rk, 611), (4, 64, 1024), jnp.float32))
        _validS = jnp.arange(1024)[None, :] < _lenS[:, None]
        _validS2 = jnp.arange(64)[None, :] < _lenS2[:, None]
        _causal = jnp.tril(jnp.ones((1024, 1024), dtype=bool))
        mask_Bx1xSxS2_ff0 = jnp.where(jnp.ones((4, 1, 1024, 64), dtype=bool), 0.0, -1000000000.0).astype(jnp.float32)
        mask_BxS2_bf1 = jnp.ones((4, 64), dtype=bool)
        return (x, ctx_2048, mask_Bx1xSxS2_ff0, mask_BxS2_bf1)
    x, ctx_2048, mask_Bx1xSxS2_ff0, mask_BxS2_bf1 = _rec_inputs()

    def _L0_xattn_setup():
        import jax, jax.numpy as jnp
        import numpy as np
        H = 1024
        NH = 32
        KVH = 8
        HD = H // NH
        GROUPS = NH // KVH
        EPS = 1e-06
        B, L, S = (4, 512, 512)

        def _gqa_forward(hidden_state, encoder_hidden_state, encoder_attention_mask, Wq, bq, Wk, bk, Wv, bv, Wo, bo, gamma, beta):
            b, l, _ = hidden_state.shape
            s = encoder_hidden_state.shape[1]
            q = hidden_state @ Wq + bq
            k = encoder_hidden_state @ Wk + bk
            v = encoder_hidden_state @ Wv + bv
            q = q.reshape(b, l, KVH, GROUPS, HD).transpose(0, 2, 3, 1, 4)
            k = k.reshape(b, s, KVH, HD).transpose(0, 2, 1, 3)
            v = v.reshape(b, s, KVH, HD).transpose(0, 2, 1, 3)
            scale = 1.0 / jnp.sqrt(jnp.asarray(HD, q.dtype))
            scores = jnp.einsum('bkgld,bksd->bkgls', q, k) * scale
            scores = scores + encoder_attention_mask[:, :, None, :, :]
            attn = jax.nn.softmax(scores, axis=-1)
            out = jnp.einsum('bkgls,bksd->bkgld', attn, v)
            out = out.transpose(0, 3, 1, 2, 4).reshape(b, l, H)
            out = out @ Wo + bo
            x = out + hidden_state
            mu = jnp.mean(x, axis=-1, keepdims=True)
            var = jnp.var(x, axis=-1, keepdims=True)
            return (x - mu) * jax.lax.rsqrt(var + EPS) * gamma + beta
        key = jax.random.key(seed)
        ks = jax.random.split(key, 12)
        sd = 0.02
        return {'hidden_state': jax.random.normal(ks[0], (B, L, H), jnp.float32), 'encoder_hidden_state': jax.random.normal(ks[1], (B, S, H), jnp.float32), 'encoder_attention_mask': jnp.zeros((B, 1, L, S), jnp.float32), 'Wq': jax.random.normal(ks[2], (H, H), jnp.float32) * sd, 'bq': jnp.zeros((H,), jnp.float32), 'Wk': jax.random.normal(ks[3], (H, KVH * HD), jnp.float32) * sd, 'bk': jnp.zeros((KVH * HD,), jnp.float32), 'Wv': jax.random.normal(ks[4], (H, KVH * HD), jnp.float32) * sd, 'bv': jnp.zeros((KVH * HD,), jnp.float32), 'Wo': jax.random.normal(ks[5], (H, H), jnp.float32) * sd, 'bo': jnp.zeros((H,), jnp.float32), 'gamma': jnp.ones((H,), jnp.float32), 'beta': jnp.zeros((H,), jnp.float32)}
    _L0_xattn_all = _L0_xattn_setup()
    _L0_xattn_in = {k: v for k, v in _L0_xattn_all.items() if k in ('Wq', 'bq', 'Wk', 'bk', 'Wv', 'bv', 'Wo', 'bo', 'gamma', 'beta')}
    del _L0_xattn_all

    def _L1_xattn_setup():
        import jax, jax.numpy as jnp
        import numpy as np
        HIDDEN = 1024
        HEADS = 16
        HEAD_DIM = HIDDEN // HEADS
        LN_EPS = 1e-05
        GATE_INIT = 0.5

        def _layer_norm(x, gamma, beta):
            mu = jnp.mean(x, axis=-1, keepdims=True)
            var = jnp.mean(jnp.square(x - mu), axis=-1, keepdims=True)
            return (x - mu) * jax.lax.rsqrt(var + LN_EPS) * gamma + beta
        key = jax.random.key(seed)
        ks = jax.random.split(key, 8)
        B, T_TEXT, T_AUDIO = (4, 1024, 750)
        s = 0.02
        return {'hidden_states': jax.random.normal(ks[0], (B, T_TEXT, HIDDEN), jnp.float32), 'audio_kv': jax.random.normal(ks[1], (B, T_AUDIO, HIDDEN), jnp.float32), 'audio_attention_mask': jnp.ones((B, T_AUDIO), dtype=bool), 'Wq': jax.random.normal(ks[2], (HIDDEN, HIDDEN), jnp.float32) * s, 'Wk': jax.random.normal(ks[3], (HIDDEN, HIDDEN), jnp.float32) * s, 'Wv': jax.random.normal(ks[4], (HIDDEN, HIDDEN), jnp.float32) * s, 'Wo': jax.random.normal(ks[5], (HIDDEN, HIDDEN), jnp.float32) * s, 'ln_gamma': jnp.ones((HIDDEN,), jnp.float32), 'ln_beta': jnp.zeros((HIDDEN,), jnp.float32), 'gate': jnp.array([GATE_INIT], jnp.float32)}
    _L1_xattn_all = _L1_xattn_setup()
    _L1_xattn_in = {k: v for k, v in _L1_xattn_all.items() if k in ('Wq', 'Wk', 'Wv', 'Wo', 'ln_gamma', 'ln_beta', 'gate')}
    del _L1_xattn_all
    return {'x': x, 'ctx_2048': ctx_2048, 'mask_Bx1xSxS2_ff0': mask_Bx1xSxS2_ff0, 'mask_BxS2_bf1': mask_BxS2_bf1, 'L0_xattn_Wq': _L0_xattn_in['Wq'], 'L0_xattn_bq': _L0_xattn_in['bq'], 'L0_xattn_Wk': _L0_xattn_in['Wk'], 'L0_xattn_bk': _L0_xattn_in['bk'], 'L0_xattn_Wv': _L0_xattn_in['Wv'], 'L0_xattn_bv': _L0_xattn_in['bv'], 'L0_xattn_Wo': _L0_xattn_in['Wo'], 'L0_xattn_bo': _L0_xattn_in['bo'], 'L0_xattn_gamma': _L0_xattn_in['gamma'], 'L0_xattn_beta': _L0_xattn_in['beta'], 'L1_xattn_Wq': _L1_xattn_in['Wq'], 'L1_xattn_Wk': _L1_xattn_in['Wk'], 'L1_xattn_Wv': _L1_xattn_in['Wv'], 'L1_xattn_Wo': _L1_xattn_in['Wo'], 'L1_xattn_ln_gamma': _L1_xattn_in['ln_gamma'], 'L1_xattn_ln_beta': _L1_xattn_in['ln_beta'], 'L1_xattn_gate': _L1_xattn_in['gate']}

def reference(x, ctx_2048, mask_Bx1xSxS2_ff0, mask_BxS2_bf1, L0_xattn_Wq, L0_xattn_bq, L0_xattn_Wk, L0_xattn_bk, L0_xattn_Wv, L0_xattn_bv, L0_xattn_Wo, L0_xattn_bo, L0_xattn_gamma, L0_xattn_beta, L1_xattn_Wq, L1_xattn_Wk, L1_xattn_Wv, L1_xattn_Wo, L1_xattn_ln_gamma, L1_xattn_ln_beta, L1_xattn_gate):
    import jax
    import jax.numpy as jnp

    def _L0_xattn_ref(hidden_state, encoder_hidden_state, encoder_attention_mask, Wq, bq, Wk, bk, Wv, bv, Wo, bo, gamma, beta):
        import jax, jax.numpy as jnp
        import numpy as np
        H = 1024
        NH = 32
        KVH = 8
        HD = H // NH
        GROUPS = NH // KVH
        EPS = 1e-06
        B, L, S = (4, 512, 512)

        def _gqa_forward(hidden_state, encoder_hidden_state, encoder_attention_mask, Wq, bq, Wk, bk, Wv, bv, Wo, bo, gamma, beta):
            b, l, _ = hidden_state.shape
            s = encoder_hidden_state.shape[1]
            q = hidden_state @ Wq + bq
            k = encoder_hidden_state @ Wk + bk
            v = encoder_hidden_state @ Wv + bv
            q = q.reshape(b, l, KVH, GROUPS, HD).transpose(0, 2, 3, 1, 4)
            k = k.reshape(b, s, KVH, HD).transpose(0, 2, 1, 3)
            v = v.reshape(b, s, KVH, HD).transpose(0, 2, 1, 3)
            scale = 1.0 / jnp.sqrt(jnp.asarray(HD, q.dtype))
            scores = jnp.einsum('bkgld,bksd->bkgls', q, k) * scale
            scores = scores + encoder_attention_mask[:, :, None, :, :]
            attn = jax.nn.softmax(scores, axis=-1)
            out = jnp.einsum('bkgls,bksd->bkgld', attn, v)
            out = out.transpose(0, 3, 1, 2, 4).reshape(b, l, H)
            out = out @ Wo + bo
            x = out + hidden_state
            mu = jnp.mean(x, axis=-1, keepdims=True)
            var = jnp.var(x, axis=-1, keepdims=True)
            return (x - mu) * jax.lax.rsqrt(var + EPS) * gamma + beta
        return _gqa_forward(hidden_state, encoder_hidden_state, encoder_attention_mask, Wq, bq, Wk, bk, Wv, bv, Wo, bo, gamma, beta)

    def _L1_xattn_ref(hidden_states, audio_kv, audio_attention_mask, Wq, Wk, Wv, Wo, ln_gamma, ln_beta, gate):
        import jax, jax.numpy as jnp
        import numpy as np
        HIDDEN = 1024
        HEADS = 16
        HEAD_DIM = HIDDEN // HEADS
        LN_EPS = 1e-05
        GATE_INIT = 0.5

        def _layer_norm(x, gamma, beta):
            mu = jnp.mean(x, axis=-1, keepdims=True)
            var = jnp.mean(jnp.square(x - mu), axis=-1, keepdims=True)
            return (x - mu) * jax.lax.rsqrt(var + LN_EPS) * gamma + beta
        B, Tt, D = hidden_states.shape
        Ta = audio_kv.shape[1]
        scale = HEAD_DIM ** (-0.5)
        a = _layer_norm(audio_kv, ln_gamma, ln_beta)
        Q = (hidden_states @ Wq.T).reshape(B, Tt, HEADS, HEAD_DIM).transpose(0, 2, 1, 3)
        K = (a @ Wk.T).reshape(B, Ta, HEADS, HEAD_DIM).transpose(0, 2, 1, 3)
        V = (a @ Wv.T).reshape(B, Ta, HEADS, HEAD_DIM).transpose(0, 2, 1, 3)
        scores = jnp.einsum('bhtd,bhsd->bhts', Q, K) * scale
        mask = audio_attention_mask[:, None, None, :]
        scores = jnp.where(mask, scores, jnp.float32(-jnp.inf))
        attn = jax.nn.softmax(scores, axis=-1)
        out = jnp.einsum('bhts,bhsd->bhtd', attn, V)
        out = out.transpose(0, 2, 1, 3).reshape(B, Tt, D)
        out = out @ Wo.T
        return hidden_states + jnp.tanh(gate) * out
    x = _L0_xattn_ref(x, ctx_2048, mask_Bx1xSxS2_ff0, L0_xattn_Wq, L0_xattn_bq, L0_xattn_Wk, L0_xattn_bk, L0_xattn_Wv, L0_xattn_bv, L0_xattn_Wo, L0_xattn_bo, L0_xattn_gamma, L0_xattn_beta)
    x = _L1_xattn_ref(x, ctx_2048, mask_BxS2_bf1, L1_xattn_Wq, L1_xattn_Wk, L1_xattn_Wv, L1_xattn_Wo, L1_xattn_ln_gamma, L1_xattn_ln_beta, L1_xattn_gate)
    return x

_drawn_inputs = setup_inputs


def setup_inputs(seed=0):
    import zlib

    import numpy as np

    out = dict(_drawn_inputs(seed))
    spreads = {'L0_xattn_bq': (0.0, 0.8),
     'L0_xattn_bk': (0.0, 0.8),
     'L0_xattn_bv': (0.0, 0.1),
     'L0_xattn_bo': (0.0, 0.1),
     'L0_xattn_gamma': (1.0, 0.2),
     'L0_xattn_beta': (0.0, 0.1),
     'L1_xattn_ln_gamma': (1.0, 0.6),
     'L1_xattn_ln_beta': (0.0, 0.449)}
    factors = {'L1_xattn_Wq': 3.677, 'L1_xattn_Wk': 3.664}
    for name, (base, spread) in spreads.items():
        noise = np.random.default_rng([zlib.crc32(name.encode()), seed]).standard_normal(out[name].shape)
        drawn = base * np.exp(spread * noise) if base else spread * noise
        out[name] = jnp.asarray(drawn.astype(out[name].dtype))
    for name, factor in factors.items():
        out[name] = (out[name] * factor).astype(out[name].dtype)
    return out
```

```python
from contextlib import ExitStack

import concourse.bass as bass
from concourse import mybir

F32 = mybir.dt.float32
F32R = mybir.dt.float32r
U8 = mybir.dt.uint8
ALU = mybir.AluOpType
ACT = mybir.ActivationFunctionType
AX_X = mybir.AxisListType.X

P = 128
BATCH, SEQ, D = 4, 1024, 1024
KEYS = 64
TOKENS = BATCH * SEQ
KT = D // P
BLK = 512
NBLK = TOKENS // BLK
TPB = BLK // P
NTILE = TOKENS // P
HALF = 512
H0, KVH0 = 32, 8
HD0 = D // H0
GRP = H0 // KVH0
KV0 = KVH0 * HD0
H1 = 16
HD1 = D // H1
SCALE0 = float(HD0) ** -0.5
SCALE1 = float(HD1) ** -0.5
EPS0, EPS1 = 1e-6, 1e-5
CTX = BATCH * KEYS


def f32(ap):
    return ap.bitcast(F32)


def three(nc, out, a, b, start, stop):
    nc.tensor.matmul(out, a[1], b[0], start=start, stop=False)
    nc.tensor.matmul(out, a[0], b[1], start=False, stop=False)
    return nc.tensor.matmul(out, a[0], b[0], start=False, stop=stop)


def row(ap, n):
    return ap.rearrange("(o n) -> o n", o=1).to_broadcast([P, n])


def context_tables(nc, ps, ident, normT, ctx_d, w, kbd_d, vbd_d):
    with ExitStack() as mem:
        def sb(name, shape, dt=F32):
            return mem.enter_context(nc.sbuf_tensor(name, shape, dt))

        def sem(name):
            return mem.enter_context(nc.semaphore(name))

        ctx = sb("ctx", [P, 2, D])
        ctxn = sb("ctxn", [P, 2, D])
        ctxT = [sb(f"ctxT{x}", [P, KT, CTX], F32R) for x in "hl"]
        wkv0 = [sb(f"wkv0{i}", [P, KT, KV0]) for i in range(2)]
        wk0 = [sb(f"wk0{x}", [P, KT, KV0], F32R) for x in "hl"]
        wv0 = [sb(f"wv0{x}", [P, KT, KV0], F32R) for x in "hl"]
        wk4 = [[sb(f"wk4{x}{i}", [P, KT, P], F32R) for x in "hl"] for i in range(2)]
        ctx2 = [[sb(f"ctx2{x}{i}", [P, KT, P], F32R) for x in "hl"] for i in range(2)]
        bk4 = sb("bk4", [P, KVH0])
        bv = sb("bv", [P, KV0])
        gam = sb("gam1", [P, D])
        bet = sb("bet1", [P, D])
        kbd = [sb(f"kbd{i}", [P, BATCH, 2, GRP, KEYS], F32R) for i in range(2)]
        vf = sb("vf", [P, KV0])
        vbd = sb("vbd", [P, KVH0, 2, 2, P], F32R)
        st = sb("ctx_st", [P, 2, 2, 6])
        mv = sb("ctx_mv", [P, 2, 2])
        rstd = sb("ctx_rstd", [P, 2, 1])
        nbias = sb("ctx_nbias", [P, 2, 1])
        mhalf = sb("mhalf", [P, 1])

        loaded, wloaded = sem("c_loaded"), sem("c_wloaded")
        zeroed = sem("c_zeroed")
        ctx_t, ctx_hi, ctx_lo = sem("c_ctx_t"), sem("c_ctx_hi"), sem("c_ctx_lo")
        stats, aggr, coef, applied, scaled, normed = (sem("c_" + n) for n in
                                                      ("stats", "aggr", "coef", "applied", "scaled", "normed"))
        wk_hi, wk_lo, w4_hi, w4_lo = sem("c_wk_hi"), sem("c_wk_lo"), sem("c_w4_hi"), sem("c_w4_lo")
        c2_hi, c2_lo = sem("c_c2_hi"), sem("c_c2_lo")
        k_done, kb_hi, kb_lo = sem("c_k_done"), sem("c_kb_hi"), sem("c_kb_lo")
        kb_out = [sem(f"c_kb_out{i}") for i in range(2)]
        v_done, v_copied, vb_hi, vb_lo, vb_out = (sem("c_" + n) for n in
                                                  ("v_done", "v_copied", "vb_hi", "vb_lo", "vb_out"))

        with nc.Block() as block:
            @block.sync
            def _(sp):
                sp.dma_start(ctx[:], ctx_d.rearrange("(r p) d -> p r d", p=P)).then_inc(loaded, 16)
                sp.dma_start(wkv0[0][:], w["Wk0"].rearrange("(k p) n -> p k n", p=P)).then_inc(wloaded, 16)
                sp.dma_start(wkv0[1][:], w["Wv0"].rearrange("(k p) n -> p k n", p=P)).then_inc(wloaded, 16)
                for j in range(GRP):
                    sp.dma_start(bk4[HD0 * j:HD0 * (j + 1), :],
                                 w["bk0"].rearrange("(g d) -> d g", d=HD0), allow_slow_non_contiguous=True)\
                        .then_inc(loaded, 16)
                sp.dma_start(bv[:], row(w["bv0"], KV0)).then_inc(loaded, 16)
                sp.dma_start(gam[:], row(w["gamma1"], D)).then_inc(loaded, 16)
                sp.dma_start(bet[:], row(w["beta1"], D)).then_inc(loaded, 16)
                for g in range(KVH0):
                    sp.wait_ge(kb_hi, g + 1)
                    sp.wait_ge(kb_lo, g + 1)
                    sp.dma_start(kbd_d[:, g].rearrange("b p c -> p b c"),
                                 f32(kbd[g % 2][:]).rearrange("p b x j s -> p b (x j s)")).then_inc(kb_out[g % 2], 16)
                for b in range(BATCH):
                    sp.wait_ge(vb_hi, b + 1)
                    sp.wait_ge(vb_lo, b + 1)
                    sp.dma_start(vbd_d[b].rearrange("g p c -> p g c"),
                                 f32(vbd[:]).rearrange("p g x u c -> p g (x u c)")).then_inc(vb_out, 16)
                for i in range(2):
                    sp.wait_ge(kb_out[i], 16 * KVH0 // 2)
                sp.wait_ge(vb_out, 16 * BATCH)

            @block.gpsimd
            def _(pool):
                nc.gpsimd.memset(ident[:], 0.0).then_inc(zeroed, 1)
                pool.wait_ge(zeroed, 1)
                nc.gpsimd.affine_select(out=ident[:], in_=ident[:], compare_op=ALU.not_equal, fill=1.0, base=0,
                                        pattern=[[-1, P]], channel_multiplier=1).then_inc(zeroed, 1)
                nc.gpsimd.memset(mhalf[:], -0.5).then_inc(zeroed, 1)
                for i in range(2):
                    nc.gpsimd.memset(f32(kbd[i][:]), 0.0).then_inc(zeroed, 1)
                nc.gpsimd.memset(f32(vbd[:]), 0.0).then_inc(zeroed, 1)
                pool.wait_ge(zeroed, 3)
                pool.wait_ge(aggr, 2)
                nc.gpsimd.tensor_scalar(rstd[:], mv[:, :, 1:2], EPS1, None, ALU.add).then_inc(coef, 1)
                pool.wait_ge(coef, 1)
                for r in range(2):
                    nc.gpsimd.tensor_tensor(rstd[:, r], rstd[:, r], mhalf[:], ALU.pow).then_inc(coef, 1)
                pool.wait_ge(coef, 3)
                for r in range(2):
                    nc.gpsimd.tensor_scalar(nbias[:, r], mv[:, r, 0:1], rstd[:, r], -1.0, ALU.mult,
                                            ALU.mult).then_inc(coef, 1)
                for r in range(2):
                    pool.wait_ge(scaled, r + 1)
                    nc.gpsimd.tensor_tensor(ctxn[:, r], ctxn[:, r], bet[:], ALU.add).then_inc(normed, 1)

            def key_hi(act, g):
                act.wait_ge(k_done, g + 1)
                act.wait_ge(loaded, 16 * 8)
                act.wait_ge(zeroed, 5)
                if g >= 2:
                    act.wait_ge(kb_out[g % 2], 16 * (g // 2))
                for j in range(GRP):
                    r = slice(HD0 * j, HD0 * (j + 1))
                    last = nc.scalar.activation(kbd[g % 2][r, :, 0, j, :], ps[r, 2048 + HALF * (g % 2):][:, :CTX]
                                                .rearrange("p (b s) -> p b s", b=BATCH), ACT.Identity,
                                                bias=bk4[r, g:g + 1])
                last.then_inc(kb_hi, 1)

            def val_hi(act, b):
                act.wait_ge(v_copied, b + 1)
                act.wait_ge(zeroed, 6)
                if b >= 1:
                    act.wait_ge(vb_out, 16 * b)
                for i in range(2):
                    r = slice(KEYS * i, KEYS * (i + 1))
                    for u in range(2):
                        c = HD0 * (2 * u + i)
                        last = nc.scalar.copy(vbd[r, :, 0, u, c:c + HD0], vf[r, :].rearrange("p (g d) -> p g d", g=KVH0))
                last.then_inc(vb_hi, 1)

            @block.scalar
            def _(act):
                act.wait_ge(ctx_t, 1)
                for i in range(4):
                    nc.scalar.copy(ctxT[0][:, 2 * i:2 * i + 2, :], ps[:, HALF * i:HALF * (i + 1)]).then_inc(ctx_hi, 1)
                act.wait_ge(wloaded, 32)
                nc.scalar.copy(wk0[0][:], wkv0[0][:]).then_inc(wk_hi, 1)
                nc.scalar.copy(wv0[0][:], wkv0[1][:]).then_inc(wk_hi, 1)
                act.wait_ge(coef, 5)
                for r in range(2):
                    nc.scalar.activation(ctxn[:, r], ctx[:, r], ACT.Identity, scale=rstd[:, r],
                                         bias=nbias[:, r]).then_inc(applied, 1)
                act.wait_ge(wk_hi, 1)
                for g in range(KVH0):
                    if g >= 2:
                        act.wait_ge(k_done, g - 1)
                    for j in range(GRP):
                        last = nc.scalar.copy(wk4[g % 2][0][:, :, HD0 * j:HD0 * (j + 1)],
                                              wkv0[0][:, :, HD0 * g:HD0 * (g + 1)])
                    last.then_inc(w4_hi, 1)
                    if g >= 1:
                        key_hi(act, g - 1)
                key_hi(act, KVH0 - 1)
                for b in range(BATCH):
                    if b >= 2:
                        act.wait_ge(v_done, b - 1)
                    for i in range(2):
                        last = nc.scalar.copy(ctx2[b % 2][0][:, :, KEYS * i:KEYS * (i + 1)],
                                              f32(ctxT[0][:, :, KEYS * b:KEYS * (b + 1)]))
                    last.then_inc(c2_hi, 1)
                    if b >= 1:
                        val_hi(act, b - 1)
                val_hi(act, BATCH - 1)
                act.wait_ge(ctx_t, 2)
                for i in range(4):
                    nc.scalar.copy(normT[0][:, 2 * i:2 * i + 2, :], ps[:, HALF * i:HALF * (i + 1)]).then_inc(ctx_hi, 1)

            @block.vector
            def _(dve):
                dve.wait_ge(loaded, 16 * 8)
                for r in range(2):
                    for n in range(2):
                        nc.vector.bn_stats(st[:, r, n], ctx[:, r, HALF * n:HALF * (n + 1)]).then_inc(stats, 1)
                dve.wait_ge(stats, 4)
                for r in range(2):
                    nc.vector.bn_aggr(mv[:, r], st[:, r]).then_inc(aggr, 1)
                for i in range(4):
                    dve.wait_ge(ctx_hi, i + 1)
                    nc.vector.tensor_tensor(ctxT[1][:, 2 * i:2 * i + 2, :], ps[:, HALF * i:HALF * (i + 1)]
                                            .rearrange("p (k c) -> p k c", k=2),
                                            f32(ctxT[0][:, 2 * i:2 * i + 2, :]), ALU.subtract).then_inc(ctx_lo, 1)
                for r in range(2):
                    dve.wait_ge(applied, r + 1)
                    nc.vector.tensor_tensor(ctxn[:, r], ctxn[:, r], gam[:], ALU.mult).then_inc(scaled, 1)
                for i, (h, l) in enumerate((wk0, wv0)):
                    dve.wait_ge(wk_hi, i + 1)
                    nc.vector.tensor_tensor(l[:], wkv0[i][:], f32(h[:]), ALU.subtract).then_inc(wk_lo, 1)
                dve.wait_ge(wk_lo, 1)

                def key_lo(g):
                    dve.wait_ge(kb_hi, g + 1)
                    for j in range(GRP):
                        r = slice(HD0 * j, HD0 * (j + 1))
                        last = nc.vector.scalar_tensor_tensor(
                            out=kbd[g % 2][r, :, 1, j, :], in0=ps[r, 2048 + HALF * (g % 2):][:, :CTX]
                            .rearrange("p (b s) -> p b s", b=BATCH), scalar=bk4[r, g:g + 1],
                            in1=f32(kbd[g % 2][r, :, 0, j, :]), op0=ALU.add, op1=ALU.subtract)
                    last.then_inc(kb_lo, 1)

                for g in range(KVH0):
                    if g >= 2:
                        dve.wait_ge(k_done, g - 1)
                    for j in range(GRP):
                        last = nc.vector.tensor_copy(wk4[g % 2][1][:, :, HD0 * j:HD0 * (j + 1)],
                                                     f32(wk0[1][:, :, HD0 * g:HD0 * (g + 1)]))
                    last.then_inc(w4_lo, 1)
                    if g >= 1:
                        key_lo(g - 1)
                key_lo(KVH0 - 1)

                def val_lo(b):
                    dve.wait_ge(v_done, b + 1)
                    if b >= 1:
                        dve.wait_ge(vb_hi, b)
                        dve.wait_ge(vb_lo, b)
                    nc.vector.tensor_tensor(vf[:], ps[:, 3072 + HALF * (b % 2):][:, :KV0], bv[:], ALU.add)\
                        .then_inc(v_copied, 1)
                    dve.wait_ge(vb_hi, b + 1)
                    dve.wait_ge(v_copied, b + 1)
                    for i in range(2):
                        r = slice(KEYS * i, KEYS * (i + 1))
                        for u in range(2):
                            c = HD0 * (2 * u + i)
                            last = nc.vector.tensor_tensor(
                                vbd[r, :, 1, u, c:c + HD0], vf[r, :].rearrange("p (g d) -> p g d", g=KVH0),
                                f32(vbd[r, :, 0, u, c:c + HD0]), ALU.subtract)
                    last.then_inc(vb_lo, 1)

                for b in range(BATCH):
                    if b >= 2:
                        dve.wait_ge(v_done, b - 1)
                    for i in range(2):
                        last = nc.vector.tensor_copy(ctx2[b % 2][1][:, :, KEYS * i:KEYS * (i + 1)],
                                                     f32(ctxT[1][:, :, KEYS * b:KEYS * (b + 1)]))
                    last.then_inc(c2_lo, 1)
                    if b >= 1:
                        val_lo(b - 1)
                val_lo(BATCH - 1)
                for i in range(4):
                    dve.wait_ge(ctx_hi, 5 + i)
                    nc.vector.tensor_tensor(normT[1][:, 2 * i:2 * i + 2, :], ps[:, HALF * i:HALF * (i + 1)]
                                            .rearrange("p (k c) -> p k c", k=2),
                                            f32(normT[0][:, 2 * i:2 * i + 2, :]), ALU.subtract).then_inc(ctx_lo, 1)

            @block.tensor
            def _(pe):
                def turn(src):
                    for k in range(KT):
                        for r in range(2):
                            last = nc.tensor.transpose(ps[:, CTX * k + P * r:][:, :P], src[:, r, P * k:P * (k + 1)],
                                                       ident[:])
                    last.then_inc(ctx_t, 1)

                pe.wait_ge(zeroed, 2)
                pe.wait_ge(loaded, 16 * 8)
                turn(ctx)
                pe.wait_ge(ctx_lo, 4)
                pe.wait_ge(ctx_hi, 4)
                pe.wait_ge(normed, 2)
                turn(ctxn)
                for g in range(KVH0):
                    pe.wait_ge(w4_hi, g + 1)
                    pe.wait_ge(w4_lo, g + 1)
                    if g >= 2:
                        pe.wait_ge(kb_lo, g - 1)
                    for k in range(KT):
                        last = three(nc, ps[:, 2048 + HALF * (g % 2):][:, :CTX], [wk4[g % 2][x][:, k] for x in (0, 1)],
                                     [ctxT[x][:, k] for x in (0, 1)], k == 0, k == KT - 1)
                    last.then_inc(k_done, 1)
                pe.wait_ge(wk_lo, 2)
                for b in range(BATCH):
                    pe.wait_ge(c2_hi, b + 1)
                    pe.wait_ge(c2_lo, b + 1)
                    if b >= 2:
                        pe.wait_ge(v_copied, b - 1)
                    for k in range(KT):
                        last = three(nc, ps[:, 3072 + HALF * (b % 2):][:, :KV0], [ctx2[b % 2][x][:, k] for x in (0, 1)],
                                     [(wv0[x])[:, k] for x in (0, 1)], k == 0, k == KT - 1)
                    last.then_inc(v_done, 1)


def layer1_tables(nc, ps, ident, normT, w, a_d, b_d):
    with ExitStack() as mem:
        def sb(name, shape, dt=F32):
            return mem.enter_context(nc.sbuf_tensor(name, shape, dt))

        def sem(name):
            return mem.enter_context(nc.semaphore(name))

        KV = range(2)
        wt = [sb(f"wt{i}", [P, D]) for i in KV]
        wq = sb("wq1", [P, D])
        wo = sb("wo1", [P, KT, P])
        wT = [[sb(f"wT{i}{x}", [P, KT, P], F32R) for x in "hl"] for i in KV]
        wqs = [sb(f"wqs{x}", [P, D], F32R) for x in "hl"]
        woT = [sb(f"woT{x}", [P, D], F32R) for x in "hl"]
        bd = [[sb(f"bd{i}{x}", [P, BATCH, 2, KEYS], F32R) for x in "hl"] for i in KV]
        ost = [sb(f"ost{i}", [P, HALF]) for i in range(4)]
        names = ("zeroed wt_loaded wq_loaded wo_loaded turned wT_hi wT_lo wo_turned wo_hi wo_lo wq_hi wq_lo "
                 "proj bd_hi bd_lo outer evac_a evac_d").split()
        s = {n: sem("l_" + n) for n in names}
        stored = [sem(f"l_stored{i}") for i in range(4)]

        with nc.Block() as block:
            @block.sync
            def _(sp):
                def pair(f, later):
                    if later:
                        sp.wait_ge(s["turned"], 2 * f)
                    sp.dma_start(wt[0][:], w["Wk1"][bass.ds(f * P, P), :]).then_inc(s["wt_loaded"], 16)
                    sp.dma_start(wt[1][:], w["Wv1"][bass.ds(f * P, P), :]).then_inc(s["wt_loaded"], 16)
                    if later:
                        sp.wait_ge(s["wq_lo"], f)
                        sp.wait_ge(s["wo_turned"], f)
                    sp.dma_start(wq[:], w["Wq1"][bass.ds(f * P, P), :]).then_inc(s["wq_loaded"], 16)
                    sp.dma_start(wo[:], w["Wo1"].rearrange("(o p) c -> p o c", p=P)[:, :, bass.ds(f * P, P)])\
                        .then_inc(s["wo_loaded"], 16)
                    for o in range(16):
                        i, e = divmod(o, 8)
                        sp.wait_ge(s["evac_d" if o % 2 else "evac_a"], 8 * f + o // 2 + 1)
                        if i == 0:
                            dst = a_d[:, P * e:P * (e + 1), :][:, :, bass.ds(f * P, P)].rearrange("b p c -> p b c")
                            src = ost[o % 4][:].rearrange("p (b c) -> p b c", b=BATCH)
                        else:
                            b, n = divmod(e, 2)
                            dst = b_d[b][bass.ds(f * P, P), :][:, HALF * n:HALF * (n + 1)]
                            src = ost[o % 4][:]
                        sp.dma_start(dst, src).then_inc(stored[o % 4], 16)
                pair(0, False)
                with sp.Fori(1, KT) as f:
                    pair(f, True)
                for i in range(4):
                    sp.wait_ge(stored[i], 16 * 4 * KT)

            def evacuate(eng, copy, odd, f, done):
                for o in range(odd, 16, 2):
                    eng.wait_ge(s["outer"], 16 * f + o + 1)
                    if not isinstance(f, int) or o >= 4:
                        eng.wait_ge(stored[o % 4], 16 * (4 * f + o // 4))
                    copy(ost[o % 4][:], ps[:, 3072 + HALF * (o % 2):][:, :HALF]).then_inc(done, 1)

            def act_pair(act, f):
                for i in KV:
                    act.wait_ge(s["turned"], 2 * f + i + 1)
                    if not isinstance(f, int) or f:
                        act.wait_ge(s["proj"], 2 * (f - 1) + i + 1)
                    nc.scalar.copy(wT[i][0][:], ps[:, D * i:D * (i + 1)]).then_inc(s["wT_hi"], 1)
                act.wait_ge(s["wq_loaded"], 16 * (f + 1))
                if not isinstance(f, int) or f:
                    act.wait_ge(s["outer"], 16 * f)
                nc.scalar.copy(wqs[0][:], wq[:]).then_inc(s["wq_hi"], 1)
                act.wait_ge(s["wo_turned"], f + 1)
                nc.scalar.copy(woT[0][:], ps[:, 0:D]).then_inc(s["wo_hi"], 1)
                act.wait_ge(s["zeroed"], 4)
                for i in KV:
                    act.wait_ge(s["proj"], 2 * f + i + 1)
                    for h in range(2):
                        r = slice(HD1 * h, HD1 * (h + 1))
                        last = nc.scalar.copy(bd[i][0][r, :, h, :], ps[r, 2048 + HALF * i:][:, :CTX]
                                              .rearrange("p (b s) -> p b s", b=BATCH))
                    last.then_inc(s["bd_hi"], 1)
                evacuate(act, nc.scalar.copy, 0, f, s["evac_a"])

            @block.scalar
            def _(act):
                act_pair(act, 0)
                with act.Fori(1, KT) as f:
                    act_pair(act, f)

            def dve_pair(dve, f):
                for i in KV:
                    dve.wait_ge(s["wT_hi"], 2 * f + i + 1)
                    nc.vector.tensor_tensor(wT[i][1][:], ps[:, D * i:D * (i + 1)].rearrange("p (k c) -> p k c", k=KT),
                                            f32(wT[i][0][:]), ALU.subtract).then_inc(s["wT_lo"], 1)
                dve.wait_ge(s["wo_hi"], f + 1)
                nc.vector.tensor_tensor(woT[1][:], ps[:, 0:D], f32(woT[0][:]), ALU.subtract).then_inc(s["wo_lo"], 1)
                for i in KV:
                    dve.wait_ge(s["bd_hi"], 2 * f + i + 1)
                    for h in range(2):
                        r = slice(HD1 * h, HD1 * (h + 1))
                        last = nc.vector.tensor_tensor(bd[i][1][r, :, h, :], ps[r, 2048 + HALF * i:][:, :CTX]
                                                       .rearrange("p (b s) -> p b s", b=BATCH),
                                                       f32(bd[i][0][r, :, h, :]), ALU.subtract)
                    last.then_inc(s["bd_lo"], 1)
                evacuate(dve, nc.vector.tensor_copy, 1, f, s["evac_d"])

            @block.vector
            def _(dve):
                dve_pair(dve, 0)
                with dve.Fori(1, KT) as f:
                    dve_pair(dve, f)

            @block.gpsimd
            def _(pool):
                for i in KV:
                    for x in range(2):
                        nc.gpsimd.memset(f32(bd[i][x][:]), 0.0).then_inc(s["zeroed"], 1)
                with pool.Fori(0, KT) as f:
                    pool.wait_ge(s["wq_hi"], f + 1)
                    nc.gpsimd.tensor_tensor(wqs[1][:], wq[:], f32(wqs[0][:]), ALU.subtract).then_inc(s["wq_lo"], 1)

            def pe_pair(pe, f):
                later = not isinstance(f, int) or f > 0
                for i in KV:
                    pe.wait_ge(s["wt_loaded"], 16 * (2 * f + 2))
                    if later and i == 0:
                        pe.wait_ge(s["wo_lo"], f)
                    for k in range(KT):
                        last = nc.tensor.transpose(ps[:, D * i + P * k:][:, :P], wt[i][:, P * k:P * (k + 1)], ident[:])
                    last.then_inc(s["turned"], 1)

                def project(i):
                    pe.wait_ge(s["wT_lo"], 2 * f + i + 1)
                    for k in range(KT):
                        last = three(nc, ps[:, 2048 + HALF * i:][:, :CTX], [wT[i][x][:, k] for x in (0, 1)],
                                     [normT[x][:, k] for x in (0, 1)], k == 0, k == KT - 1)
                    last.then_inc(s["proj"], 1)

                project(0)
                pe.wait_ge(s["wo_loaded"], 16 * (f + 1))
                for o in range(KT):
                    last = nc.tensor.transpose(ps[:, P * o:P * (o + 1)], wo[:, o, :], ident[:])
                last.then_inc(s["wo_turned"], 1)
                project(1)
                for o in range(16):
                    i, e = divmod(o, 8)
                    if o == 0:
                        pe.wait_ge(s["bd_lo"], 2 * f + 1)
                        pe.wait_ge(s["wq_lo"], f + 1)
                    if o == 8:
                        pe.wait_ge(s["bd_lo"], 2 * f + 2)
                        pe.wait_ge(s["wo_lo"], f + 1)
                    if o >= 2 or later:
                        pe.wait_ge(s["evac_d" if o % 2 else "evac_a"], 8 * f + o // 2)
                    out = ps[:, 3072 + HALF * (o % 2):][:, :HALF]
                    if i == 0:
                        a = [wqs[x][:, P * e:P * (e + 1)] for x in (0, 1)]
                        b = [bd[0][x][:].rearrange("p b h s -> p (b h s)") for x in (0, 1)]
                    else:
                        a = [bd[1][x][:, e // 2].rearrange("p h s -> p (h s)") for x in (0, 1)]
                        b = [woT[x][:, HALF * (e % 2):HALF * (e % 2 + 1)] for x in (0, 1)]
                    three(nc, out, a, b, True, True).then_inc(s["outer"], 1)

            @block.tensor
            def _(pe):
                pe_pair(pe, 0)
                with pe.Fori(1, KT) as f:
                    pe_pair(pe, f)


def q_projection(nc, ps, ident, x_d, w, q_d):
    with ExitStack() as mem:
        def sb(name, shape, dt=F32):
            return mem.enter_context(nc.sbuf_tensor(name, shape, dt))

        def sem(name):
            return mem.enter_context(nc.semaphore("q_" + name))

        wq = [sb(f"wq0{x}", [P, KT, D], F32R) for x in "hl"]
        raw = [sb(f"wraw{i}", [P, D]) for i in range(3)]
        bq = sb("bq", [P, KT])
        xt = [sb(f"xt{i}", [P, D]) for i in range(4)]
        xT = [[sb(f"xT{i}{x}", [P, KT, BLK], F32R) for x in "hl"] for i in range(2)]
        qst = [sb(f"qst{i}", [P, BLK]) for i in range(4)]
        b_loaded, w_hi, w_lo = sem("b_loaded"), sem("w_hi"), sem("w_lo")
        turned, x_hi, x_lo = sem("turned"), sem("x_hi"), sem("x_lo")
        q_done, q_out = sem("q_done"), sem("q_out")
        w_loaded = [sem(f"w_loaded{i}") for i in range(3)]
        x_loaded = [sem(f"x_loaded{i}") for i in range(4)]
        q_stored = [sem(f"q_stored{i}") for i in range(4)]

        def pairs(eng, body):
            body(0, 0, True)
            body(1, 1, True)
            with eng.Fori(1, NBLK // 2 - 1) as i:
                body(2 * i, 0, True)
                body(2 * i + 1, 1, True)
            body(NBLK - 2, 0, True)
            body(NBLK - 1, 1, False)

        with nc.Block() as block:
            @block.sync
            def _(sp):
                def load(t, m):
                    if not isinstance(t, int) or t:
                        sp.wait_ge(turned, 4 * (t - 1) + m + 1)
                    sp.dma_start(xt[m][:], x_d[bass.ds(BLK * t + P * m, P), :]).then_inc(x_loaded[m], 16)

                for m in range(TPB):
                    load(0, m)
                for k in range(KT):
                    if k >= 3:
                        sp.wait_ge(w_lo, k - 2)
                    sp.dma_start(raw[k % 3][:], w["Wq0"][P * k:P * (k + 1), :]).then_inc(w_loaded[k % 3], 16)
                sp.dma_start(bq[:], w["bq0"].rearrange("(g p) -> p g", p=P), allow_slow_non_contiguous=True)\
                    .then_inc(b_loaded, 16)

                def body(t, par, more):
                    for g in range(KT):
                        if more and g % 2 == 0:
                            load(t + 1, g // 2)
                        sp.wait_ge(q_out, 8 * t + g + 1)
                        sp.dma_start(q_d[t, g], qst[g % 4][:]).then_inc(q_stored[g % 4], 16)

                pairs(sp, body)
                for i in range(4):
                    sp.wait_ge(q_stored[i], 16 * 2 * NBLK)

            def x_hi_part(act, t, par, m):
                act.wait_ge(turned, 4 * t + m + 1)
                nc.scalar.copy(xT[par][0][:, :, P * m:P * (m + 1)], ps[:, D * (m % 2):][:, :D]
                               .rearrange("p (k c) -> p k c", k=KT)).then_inc(x_hi, 1)

            @block.scalar
            def _(act):
                for m in range(TPB):
                    x_hi_part(act, 0, 0, m)
                    for k in (2 * m, 2 * m + 1):
                        act.wait_ge(w_loaded[k % 3], 16 * (k // 3 + 1))
                        nc.scalar.copy(wq[0][:, k], raw[k % 3][:]).then_inc(w_hi, 1)
                act.wait_ge(b_loaded, 16)

                def body(t, par, more):
                    for g in range(KT):
                        if more and g % 2 == 1:
                            x_hi_part(act, t + 1, 1 - par, g // 2)
                        act.wait_ge(q_done, 8 * t + g + 1)
                        if not isinstance(t, int) or 8 * t + g >= 4:
                            act.wait_ge(q_stored[g % 4], 16 * (2 * t + g // 4))
                        nc.scalar.activation(qst[g % 4][:], ps[:, 2048 + HALF * (g % 4):][:, :HALF], ACT.Identity,
                                             bias=bq[:, g:g + 1]).then_inc(q_out, 1)

                pairs(act, body)

            def x_lo_part(dve, t, par, m):
                dve.wait_ge(x_hi, 4 * t + m + 1)
                nc.vector.tensor_tensor(xT[par][1][:, :, P * m:P * (m + 1)], ps[:, D * (m % 2):][:, :D]
                                        .rearrange("p (k c) -> p k c", k=KT),
                                        f32(xT[par][0][:, :, P * m:P * (m + 1)]), ALU.subtract).then_inc(x_lo, 1)

            @block.vector
            def _(dve):
                for m in range(TPB):
                    x_lo_part(dve, 0, 0, m)
                    for k in (2 * m, 2 * m + 1):
                        dve.wait_ge(w_hi, k + 1)
                        nc.vector.tensor_tensor(wq[1][:, k], raw[k % 3][:], f32(wq[0][:, k]), ALU.subtract)\
                            .then_inc(w_lo, 1)

                def body(t, par, more):
                    for m in range(TPB):
                        if more:
                            x_lo_part(dve, t + 1, 1 - par, m)

                pairs(dve, body)

            @block.tensor
            def _(pe):
                def turn(t, m):
                    pe.wait_ge(x_loaded[m], 16 * (t + 1))
                    if not isinstance(t, int) or 4 * t + m >= 2:
                        pe.wait_ge(x_lo, 4 * t + m - 1)
                    for k in range(KT):
                        last = nc.tensor.transpose(ps[:, D * (m % 2) + P * k:][:, :P], xt[m][:, P * k:P * (k + 1)],
                                                   ident[:])
                    last.then_inc(turned, 1)

                for m in range(TPB):
                    turn(0, m)

                def body(t, par, more):
                    pe.wait_ge(x_lo, 4 * (t + 1))
                    for g in range(KT):
                        if more and g % 2 == 1:
                            turn(t + 1, g // 2)
                        if not isinstance(t, int) or 8 * t + g >= 4:
                            pe.wait_ge(q_out, 8 * t + g - 3)
                        for k in range(KT):
                            if isinstance(t, int) and t == 0 and g == 0:
                                pe.wait_ge(w_lo, k + 1)
                            last = three(nc, ps[:, 2048 + HALF * (g % 4):][:, :HALF],
                                         [wq[x][:, k, P * g:P * (g + 1)] for x in (0, 1)],
                                         [xT[par][x][:, k] for x in (0, 1)], k == 0, k == KT - 1)
                        last.then_inc(q_done, 1)

                pairs(pe, body)


def layer0(nc, ps, ident, x_d, q_d, mask_d, kbd_d, vbd_d, w, x2_d):
    with ExitStack() as mem:
        def sb(name, shape, dt=F32):
            return mem.enter_context(nc.sbuf_tensor(name, shape, dt))

        def sem(name):
            return mem.enter_context(nc.semaphore("a_" + name))

        wo = [sb(f"wo0{x}", [P, KT, D], F32R) for x in "hl"]
        oT = [[sb(f"oT{i}{x}", [P, KT, BLK], F32R) for x in "hl"] for i in range(2)]
        kb = [sb(f"kb{i}", [P, 2, GRP * KEYS], F32R) for i in range(2)]
        vb = [sb(f"vb{i}", [P, 2, 2, P], F32R) for i in range(2)]
        qf = [sb(f"qf{i}", [P, BLK]) for i in range(2)]
        qs = [[sb(f"qs{i}{x}", [P, BLK], F32R) for x in "hl"] for i in range(2)]
        pr = [sb(f"pr{i}", [P, TPB, GRP, KEYS]) for i in range(2)]
        pT = [sb(f"pT{x}", [P, 2, BLK], F32R) for x in "hl"]
        xb = [sb(f"xb{i}", [P, D]) for i in range(2)]
        y = [sb(f"y{i}", [P, D]) for i in range(2)]
        mask = [sb(f"mask{i}", [P, TPB, KEYS]) for i in range(2)]
        gam, bet, bo = sb("gam0", [P, D]), sb("bet0", [P, D]), sb("bo0", [P, D])
        mx, sm, rs = sb("mx", [P, TPB * GRP]), sb("sm", [P, TPB * GRP]), sb("rs", [P, TPB * GRP])
        st, mv = sb("st", [P, 2, 6]), sb("mv", [P, 2])
        rstd, nbias, mhalf = sb("rstd", [P, 1]), sb("nbias", [P, 1]), sb("mhalf0", [P, 1])
        eps, minus = sb("eps", [P, 1]), sb("minus", [P, 1])

        S, T, V, O = (lambda: ps[:, 0:1024]), (lambda: ps[:, 1024:2048]), (lambda: ps[:, 2048:2560]), \
            (lambda n: ps[:, 2560 + HALF * n:][:, :HALF])

        (w_hi, w_lo, c_loaded, half_set, m_loaded, q_hi, q_lo, scores, s_read, maxed, centered, exped, summed, recips,
         probs, turned, pt_hi, pt_lo, pv, o_hi, o_lo, o_done, xbo, y_done, st_done, aggr, coef, applied, scaled,
         normed) = (sem(n) for n in (
             "w_hi w_lo c_loaded half_set m_loaded q_hi q_lo scores s_read maxed centered exped summed recips probs "
             "turned pt_hi pt_lo pv o_hi o_lo o_done xbo y_done st_done aggr coef applied scaled normed").split())
        w_loaded = [sem(f"w_loaded{i}") for i in range(4)]
        q_loaded, k_loaded, v_loaded, x_loaded, stored = (
            [sem(f"{n}{i}") for i in range(2)] for n in "q_loaded k_loaded v_loaded x_loaded stored".split())

        def blocks(eng, body):
            body(0, 0, True, False)
            body(1, 1, True, True)
            with eng.Fori(1, NBLK // 2 - 1) as i:
                body(2 * i, 0, True, True)
                body(2 * i + 1, 1, True, True)
            body(NBLK - 2, 0, True, True)
            body(NBLK - 1, 1, True, True)
            body(NBLK, 0, False, True)

        def after(t, g, n):
            return not isinstance(t, int) or 8 * t + g >= n

        def lagging(t, g):
            if g % 2 or (isinstance(t, int) and 4 * (t - 1) + g // 2 - 1 < 0):
                return None
            return 4 * (t - 1) + g // 2 - 1

        with nc.Block() as block:
            @block.sync
            def _(sp):
                def load_q(u, g):
                    sp.dma_start(qf[g % 2][:], q_d.rearrange("t g p c -> (t g) p c")[u]).then_inc(q_loaded[g % 2], 16)

                def load_k(t, g):
                    sp.dma_start(f32(kb[g % 2][:]).rearrange("p x c -> p (x c)"), kbd_d[t // 2, g])\
                        .then_inc(k_loaded[g % 2], 16)

                def load_v(t, g):
                    sp.dma_start(f32(vb[g % 2][:]).rearrange("p x u c -> p (x u c)"), vbd_d[t // 2, g])\
                        .then_inc(v_loaded[g % 2], 16)

                def load_mask(t, par):
                    sp.dma_start(mask[par][:], mask_d[bass.ds(BLK * t, BLK), :].rearrange("(m p) s -> p m s", p=P))\
                        .then_inc(m_loaded, 16)

                load_q(0, 0)
                load_k(0, 0)
                load_mask(0, 0)
                load_q(1, 1)
                load_k(0, 1)
                load_v(0, 0)
                for k in range(KT):
                    if k >= 4:
                        sp.wait_ge(w_lo, k - 3)
                    sp.dma_start((y + xb)[k % 4][:], w["Wo0"][P * k:P * (k + 1), :]).then_inc(w_loaded[k % 4], 16)
                sp.dma_start(gam[:], row(w["gamma0"], D)).then_inc(c_loaded, 16)
                sp.dma_start(bet[:], row(w["beta0"], D)).then_inc(c_loaded, 16)
                sp.dma_start(bo[:], row(w["bo0"], D)).then_inc(c_loaded, 16)

                def body(t, par, attn, proj):
                    last_t = isinstance(t, int) and t == NBLK - 1
                    for g in range(KT):
                        u = 8 * t + g
                        if attn and g == 1 and not last_t:
                            if after(t, g, 2):
                                sp.wait_ge(s_read, u - 1)
                            load_mask(t + 1, 1 - par)
                        if attn and not (last_t and g >= KT - 2):
                            g2, t2 = (g + 2) % KT, t + (g + 2) // KT
                            sp.wait_ge(q_lo, u + 1)
                            load_q(u + 2, g2)
                            sp.wait_ge(scores, u + 1)
                            load_k(t2, g2)
                        if attn and not (last_t and g == KT - 1):
                            if after(t, g, 1):
                                sp.wait_ge(pv, u)
                            load_v(t + (g + 1) // KT, (g + 1) % KT)
                        if g % 2 == 0 and ((proj and not (g == 6 and not attn)) or (g == 6 and attn)):
                            n = 4 * (t - 1) + g // 2 + 1
                            if isinstance(n, int) and n < 2:
                                sp.wait_ge(w_lo, KT)
                            else:
                                sp.wait_ge(y_done, 2 * (n - 1))
                            sp.dma_start(xb[(g // 2 + 1) % 2][:], x_d[bass.ds(P * n, P), :])\
                                .then_inc(x_loaded[(g // 2 + 1) % 2], 16)
                        if g % 2 == 1 and lagging(t, g - 1) is not None:
                            n = lagging(t, g - 1)
                            sp.wait_ge(normed, n + 1)
                            sp.dma_start(x2_d[bass.ds(P * n, P), :], y[(g // 2 + 1) % 2][:])\
                                .then_inc(stored[(g // 2 + 1) % 2], 16)

                blocks(sp, body)
                sp.wait_ge(normed, NTILE)
                sp.dma_start(x2_d[P * (NTILE - 1):P * NTILE, :], y[(NTILE - 1) % 2][:])\
                    .then_inc(stored[(NTILE - 1) % 2], 16)
                for i in range(2):
                    sp.wait_ge(stored[i], 16 * NTILE // 2)

            @block.tensor
            def _(pe):
                def output(t, par, g, fs):
                    m, n = divmod(g, 2)
                    h = 8 * (t - 1) + g
                    if fs[0] == 0:
                        if not isinstance(h, int) or h >= 2:
                            pe.wait_ge(y_done, h - 1)
                        pe.wait_ge(o_lo, 8 * t - 1)
                    elif g == 0:
                        pe.wait_ge(o_lo, 8 * t)
                    for f in fs:
                        last = three(nc, O(n), [oT[1 - par][x][:, f, P * m:P * (m + 1)] for x in (0, 1)],
                                     [wo[x][:, f, HALF * n:HALF * (n + 1)] for x in (0, 1)], f == 0, f == KT - 1)
                    if fs[-1] == KT - 1:
                        last.then_inc(o_done, 1)

                def body(t, par, attn, proj):
                    for g in range(KT):
                        u = 8 * t + g
                        prev = (attn and after(t, g, 1)) or (not attn and g == 0)
                        g1 = (g - 1) % KT
                        if attn:
                            pe.wait_ge(q_lo, u + 1)
                            pe.wait_ge(k_loaded[g % 2], 16 * (4 * t + g // 2 + 1))
                            if after(t, g, 1):
                                pe.wait_ge(s_read, u)
                            for m in range(TPB):
                                last = three(nc, S()[:, 256 * m:256 * (m + 1)],
                                             [qs[g % 2][x][:, P * m:P * (m + 1)] for x in (0, 1)],
                                             [kb[g % 2][:, x] for x in (0, 1)],
                                             True, True)
                            last.then_inc(scores, 1)
                        if prev:
                            pe.wait_ge(probs, u)
                            if after(t, g, 2):
                                pe.wait_ge(pt_lo, u - 1)
                            for c in range(2):
                                for m in range(TPB):
                                    last = nc.tensor.transpose(
                                        T()[:, BLK * c + P * m:][:, :P],
                                        pr[g1 % 2][:, m, 2 * c:2 * c + 2, :].rearrange("p j s -> p (j s)"), ident[:])
                            last.then_inc(turned, 1)
                        if proj:
                            if isinstance(t, int) and t == 1 and g == 0:
                                pe.wait_ge(w_lo, KT)
                            output(t, par, g, range(0, 4))
                        if prev:
                            pe.wait_ge(pt_lo, u)
                            pe.wait_ge(v_loaded[g1 % 2], 16 * (4 * t + (g - 1) // 2 + 1))
                            if after(t, g, 2):
                                pe.wait_ge(o_lo, u - 1)
                            for c in range(2):
                                last = three(nc, V(), [vb[g1 % 2][:, x, c] for x in (0, 1)],
                                             [pT[x][:, c] for x in (0, 1)], c == 0, c == 1)
                            last.then_inc(pv, 1)
                        if proj:
                            output(t, par, g, range(4, KT))

                blocks(pe, body)

            @block.scalar
            def _(act):
                def split_q(t, g):
                    u = 8 * t + g
                    act.wait_ge(q_loaded[g % 2], 16 * (4 * t + g // 2 + 1))
                    if after(t, g, 2):
                        act.wait_ge(scores, u - 1)
                    nc.scalar.copy(qs[g % 2][0][:], qf[g % 2][:]).then_inc(q_hi, 1)

                for k in range(KT):
                    act.wait_ge(w_loaded[k % 4], 16 * (k // 4 + 1))
                    nc.scalar.copy(wo[0][:, k], (y + xb)[k % 4][:]).then_inc(w_hi, 1)
                split_q(0, 0)

                def body(t, par, attn, proj):
                    for g in range(KT):
                        u = 8 * t + g
                        prev = (attn and after(t, g, 1)) or (not attn and g == 0)
                        if attn and not (isinstance(t, int) and t == NBLK - 1 and g == KT - 1):
                            split_q(t, g + 1)
                        if prev:
                            act.wait_ge(turned, u)
                            if after(t, g, 2):
                                act.wait_ge(pv, u - 1)
                            nc.scalar.copy(pT[0][:].rearrange("p c n -> p (c n)"), T()).then_inc(pt_hi, 1)
                        n = lagging(t, g)
                        if n is not None:
                            act.wait_ge(coef, 4 * (n + 1))
                            yb = y[(g // 2 + 1) % 2]
                            nc.scalar.activation(yb[:], yb[:], ACT.Identity, scale=rstd[:], bias=nbias[:])\
                                .then_inc(applied, 1)
                        if attn:
                            act.wait_ge(centered, u + 1)
                            e = pr[g % 2][:].rearrange("p m j s -> p (m j s)")
                            nc.scalar.activation(e, e, ACT.Exp).then_inc(exped, 1)
                        if prev:
                            act.wait_ge(pv, u)
                            op = par if g else 1 - par
                            nc.scalar.copy(oT[op][0][:, (g - 1) % KT], V()).then_inc(o_hi, 1)

                blocks(act, body)
                act.wait_ge(coef, 4 * NTILE)
                yb = y[(NTILE - 1) % 2]
                nc.scalar.activation(yb[:], yb[:], ACT.Identity, scale=rstd[:], bias=nbias[:]).then_inc(applied, 1)

            @block.vector
            def _(dve):
                for k in range(KT):
                    dve.wait_ge(w_hi, k + 1)
                    nc.vector.tensor_tensor(wo[1][:, k], (y + xb)[k % 4][:], f32(wo[0][:, k]), ALU.subtract)\
                        .then_inc(w_lo, 1)

                def scale_by_gamma(n, yb):
                    dve.wait_ge(applied, n + 1)
                    nc.vector.tensor_tensor(yb[:], yb[:], gam[:], ALU.mult).then_inc(scaled, 1)

                def statistics_ready(n):
                    dve.wait_ge(st_done, 2 * (n + 1))
                    if not isinstance(n, int) or n:
                        dve.wait_ge(coef, 4 * n)

                dve.wait_ge(c_loaded, 48)

                def body(t, par, attn, proj):
                    for g in range(KT):
                        u = 8 * t + g
                        prev = (attn and after(t, g, 1)) or (not attn and g == 0)
                        p = pr[g % 2]
                        heads = p[:].rearrange("p m j s -> p (m j) s")
                        n = lagging(t, g)
                        if n is not None and not attn:
                            statistics_ready(n)
                            nc.vector.bn_aggr(mv[:], st[:]).then_inc(aggr, 1)
                        if attn:
                            dve.wait_ge(scores, u + 1)
                            if g == 0:
                                dve.wait_ge(m_loaded, 16 * (t + 1))
                            if after(t, g, 2):
                                dve.wait_ge(turned, u - 1)
                            if n is not None:
                                statistics_ready(n)
                            for m in range(TPB):
                                last = nc.vector.scalar_tensor_tensor(
                                    out=p[:, m], in0=S()[:, 256 * m:256 * (m + 1)]
                                    .rearrange("p (j s) -> p j s", j=GRP), scalar=SCALE0,
                                    in1=mask[par][:, m, :].unsqueeze(1).to_broadcast([P, GRP, KEYS]),
                                    op0=ALU.mult, op1=ALU.add)
                            last.then_inc(s_read, 1)
                            if n is not None:
                                nc.vector.bn_aggr(mv[:], st[:]).then_inc(aggr, 1)
                            dve.wait_ge(s_read, u + 1)
                            if after(t, g, 1):
                                dve.wait_ge(centered, u)
                            nc.vector.tensor_reduce(mx[:], heads, AX_X, ALU.max).then_inc(maxed, 1)
                        if prev:
                            dve.wait_ge(pt_hi, u)
                            nc.vector.tensor_tensor(pT[1][:].rearrange("p c n -> p (c n)"), T(),
                                                    f32(pT[0][:]).rearrange("p c n -> p (c n)"), ALU.subtract)\
                                .then_inc(pt_lo, 1)
                        if n is not None:
                            scale_by_gamma(n, y[(g // 2 + 1) % 2])
                        if attn:
                            dve.wait_ge(exped, u + 1)
                            nc.vector.tensor_reduce(sm[:], heads, AX_X, ALU.add).then_inc(summed, 1)
                            dve.wait_ge(summed, u + 1)
                            if after(t, g, 1):
                                dve.wait_ge(probs, u)
                            nc.vector.reciprocal(rs[:], sm[:]).then_inc(recips, 1)
                        if prev:
                            dve.wait_ge(o_hi, u)
                            op = par if g else 1 - par
                            g1 = (g - 1) % KT
                            nc.vector.tensor_tensor(oT[op][1][:, g1], V(), f32(oT[op][0][:, g1]), ALU.subtract)\
                                .then_inc(o_lo, 1)
                        if proj:
                            h = 8 * (t - 1) + g
                            m, half = divmod(g, 2)
                            cols = slice(HALF * half, HALF * (half + 1))
                            dve.wait_ge(o_done, h + 1)
                            dve.wait_ge(xbo, h // 2 + 1 if isinstance(h, int) else 4 * (t - 1) + m + 1)
                            if half == 0 and (not isinstance(t, int) or 4 * (t - 1) + m >= 2):
                                dve.wait_ge(stored[m % 2], 16 * (2 * (t - 1) + m // 2))
                            nc.vector.tensor_tensor(y[m % 2][:, cols], O(half), xb[m % 2][:, cols], ALU.add)\
                                .then_inc(y_done, 1)
                            dve.wait_ge(y_done, h + 1)
                            nc.vector.bn_stats(st[:, half], y[m % 2][:, cols]).then_inc(st_done, 1)

                blocks(dve, body)
                statistics_ready(NTILE - 1)
                nc.vector.bn_aggr(mv[:], st[:]).then_inc(aggr, 1)
                scale_by_gamma(NTILE - 1, y[(NTILE - 1) % 2])

            @block.gpsimd
            def _(pool):
                nc.gpsimd.memset(mhalf[:], -0.5).then_inc(half_set, 1)
                nc.gpsimd.memset(eps[:], EPS0).then_inc(half_set, 1)
                nc.gpsimd.memset(minus[:], -1.0).then_inc(half_set, 1)
                pool.wait_ge(half_set, 3)
                pool.wait_ge(c_loaded, 48)

                def split_q(u, g):
                    pool.wait_ge(q_hi, u + 1)
                    nc.gpsimd.tensor_tensor(qs[g % 2][1][:], qf[g % 2][:], f32(qs[g % 2][0][:]), ALU.subtract)\
                        .then_inc(q_lo, 1)

                def coefficients(n):
                    pool.wait_ge(aggr, n + 1)
                    if not isinstance(n, int) or n >= 1:
                        pool.wait_ge(applied, n)
                    nc.gpsimd.tensor_tensor(rstd[:], mv[:, 1:2], eps[:], ALU.add).then_inc(coef, 1)
                    nc.gpsimd.tensor_tensor(nbias[:], mv[:, 0:1], minus[:], ALU.mult).then_inc(coef, 1)
                    pool.wait_ge(coef, 4 * n + 2)
                    nc.gpsimd.tensor_tensor(rstd[:], rstd[:], mhalf[:], ALU.pow).then_inc(coef, 1)
                    pool.wait_ge(coef, 4 * n + 3)
                    nc.gpsimd.tensor_tensor(nbias[:], nbias[:], rstd[:], ALU.mult).then_inc(coef, 1)

                def shift_by_beta(n, yb):
                    pool.wait_ge(scaled, n + 1)
                    nc.gpsimd.tensor_tensor(yb[:], yb[:], bet[:], ALU.add).then_inc(normed, 1)

                split_q(0, 0)

                def body(t, par, attn, proj):
                    for g in range(KT):
                        u = 8 * t + g
                        heads = pr[g % 2][:].rearrange("p m j s -> p (m j) s")
                        n = lagging(t, g)
                        if n is not None:
                            coefficients(n)
                        if attn and not (isinstance(t, int) and t == NBLK - 1 and g == KT - 1):
                            split_q(u + 1, g + 1)
                        if attn:
                            pool.wait_ge(maxed, u + 1)
                            nc.gpsimd.tensor_tensor(heads, heads, mx[:].unsqueeze(2).to_broadcast([P, TPB * GRP, KEYS]),
                                                    ALU.subtract).then_inc(centered, 1)
                        if n is not None:
                            shift_by_beta(n, y[(g // 2 + 1) % 2])
                        if g % 2 == 1 and ((proj and not (g == 7 and not attn)) or (g == 7 and attn)):
                            r = 4 * (t - 1) + g // 2 + 1
                            pool.wait_ge(x_loaded[(g // 2 + 1) % 2], 16 * (2 * (t - 1) + (g // 2 + 1) // 2 + 1))
                            xr = xb[(g // 2 + 1) % 2]
                            nc.gpsimd.tensor_tensor(xr[:], xr[:], bo[:], ALU.add).then_inc(xbo, 1)
                        if attn:
                            pool.wait_ge(recips, u + 1)
                            nc.gpsimd.tensor_tensor(heads, heads, rs[:].unsqueeze(2).to_broadcast([P, TPB * GRP, KEYS]),
                                                    ALU.mult).then_inc(probs, 1)

                blocks(pool, body)
                coefficients(NTILE - 1)
                shift_by_beta(NTILE - 1, y[(NTILE - 1) % 2])


def layer1(nc, ps, ident, x2_d, kmask_d, gate_d, a_d, b_d, out_d):
    M = SEQ // P
    with ExitStack() as mem:
        def sb(name, shape, dt=F32):
            return mem.enter_context(nc.sbuf_tensor(name, shape, dt))

        def sem(name):
            return mem.enter_context(nc.semaphore("b_" + name))

        A = [sb(f"A{x}", [P, KT, D], F32R) for x in "hl"]
        B = [sb(f"B{x}", [P, KT, D], F32R) for x in "hl"]
        raw = [sb(f"raw{i}", [P, D]) for i in range(8)]
        xt = [sb(f"x2t{i}", [P, D]) for i in range(4)]
        xT = [sb(f"x2T{x}", [P, KT, P], F32R) for x in "hl"]
        pr = sb("prob", [P, H1, KEYS])
        pT = [sb(f"probT{x}", [P, KT, P], F32R) for x in "hl"]
        km = sb("km", [P, BATCH, KEYS], U8)
        bias = sb("bias", [P, BATCH, KEYS])
        zero = sb("zero", [P, BATCH, KEYS])
        gate, gt = sb("gate", [P, 1]), sb("gt", [P, 1])
        mx, sm, rs = sb("mx1", [P, H1]), sb("sm1", [P, H1]), sb("rs1", [P, H1])

        (c_loaded, set_, masked, gated, a_hi, a_loe, a_loo, b_hi, b_loe, b_loo, a_free, b_free, x_turned, x_hi, x_lo,
         scores, s_read, maxed, centered, exped, summed, recips, probs, p_turned, p_hi, p_lo, o_done,
         out_done) = (sem(n) for n in (
             "c_loaded set masked gated a_hi a_loe a_loo b_hi b_loe b_loo a_free b_free x_turned x_hi x_lo scores "
             "s_read maxed centered exped summed recips probs p_turned p_hi p_lo o_done out_done").split())
        ab_loaded = [sem(f"ab_loaded{i}") for i in range(8)]
        x_loaded = [sem(f"x_loaded{i}") for i in range(4)]
        stored = [sem(f"stored{i}") for i in range(4)]
        S, XT, PT, O = (lambda: ps[:, 0:1024]), (lambda: ps[:, 1024:2048]), (lambda: ps[:, 2048:3072]), \
            (lambda n: ps[:, 3072 + HALF * n:][:, :HALF])

        def batches(eng, slot):
            slot(0, 0, False)
            with eng.Fori(0, BATCH - 1) as b:
                for m in range(1, M):
                    slot(b, m, False)
                slot(b + 1, 0, False)
            for m in range(1, M):
                slot(BATCH - 1, m, True)

        def after(b, m, n):
            return not isinstance(b, int) or M * b + m >= n

        def hi(act, dst, c, b, first):
            k = c % KT
            act.wait_ge(ab_loaded[k], 16 * (2 * b + c // KT + 1))
            if not first:
                if k < KT - 1:
                    act.wait_ge(a_free if c < KT else b_free, (KT - 1) * (b - 1) + k + 1)
                elif c < KT:
                    act.wait_ge(scores, M * b)
                else:
                    act.wait_ge(o_done, 2 * M * b)
            nc.scalar.copy(dst[0][:, k], raw[k][:]).then_inc(a_hi if c < KT else b_hi, 1)

        def lo(eng, sub, dst, c, b):
            k = c % KT
            eng.wait_ge(a_hi if c < KT else b_hi, KT * b + k + 1)
            done = (a_loo if k % 2 else a_loe) if c < KT else (b_loo if k % 2 else b_loe)
            sub(dst[1][:, k], raw[k][:], f32(dst[0][:, k]), ALU.subtract).then_inc(done, 1)

        with nc.Block() as block:
            @block.sync
            def _(sp):
                def load_x(u, i):
                    sp.dma_start(xt[i][:], x2_d[bass.ds(P * u, P), :]).then_inc(x_loaded[i], 16)

                def load_ab(b, c, first):
                    k = c % KT
                    if not first:
                        before = (b if c >= KT else b - 1)
                        odd, even = (a_loo, a_loe) if c >= KT else (b_loo, b_loe)
                        sp.wait_ge(odd if k % 2 else even, KT // 2 * before + k // 2 + 1)
                    src = a_d if c < KT else b_d
                    sp.dma_start(raw[k][:], src[b][P * k:P * (k + 1), :]).then_inc(ab_loaded[k], 16)

                load_x(0, 0)
                sp.dma_start(km[:], kmask_d.rearrange("b s -> (b s)").rearrange("(o n) -> o n", o=1)
                             .to_broadcast([P, BATCH * KEYS])).then_inc(c_loaded, 16)
                sp.dma_start(gate[:], gate_d.rearrange("(o n) -> o n", o=1).to_broadcast([P, 1])).then_inc(c_loaded, 16)
                for c in range(KT):
                    load_ab(0, c, True)
                for i in range(1, 4):
                    load_x(i, i)
                for c in range(KT, 2 * KT):
                    load_ab(0, c, False)

                def slot(b, m, last):
                    u = M * b + m
                    if m == 2 and not last:
                        for c in range(KT):
                            load_ab(b + 1, c, False)
                    if m == 0 and (not isinstance(b, int) or b):
                        for c in range(KT, 2 * KT):
                            load_ab(b, c, False)
                    if after(b, m, 1):
                        sp.wait_ge(out_done, 2 * u)
                        sp.dma_start(out_d[bass.ds(P * (u - 1), P), :], xt[(m - 1) % 4][:])\
                            .then_inc(stored[(m - 1) % 4], 16)
                        if not (last and m >= M - 3):
                            sp.wait_ge(stored[(m - 1) % 4], 16 * (2 * b + (m - 1) // 4 + 1))
                            load_x(u + 3, (m + 3) % 4)

                batches(sp, slot)
                sp.wait_ge(out_done, 2 * NTILE)
                sp.dma_start(out_d[P * (NTILE - 1):P * NTILE, :], xt[(NTILE - 1) % 4][:])\
                    .then_inc(stored[(NTILE - 1) % 4], 16)
                for i in range(4):
                    sp.wait_ge(stored[i], 16 * NTILE // 4)

            @block.tensor
            def _(pe):
                def turn_x(b, m):
                    u, i = M * b + m, m % 4
                    pe.wait_ge(x_loaded[i], 16 * (2 * b + m // 4 + 1))
                    if after(b, m, 1):
                        pe.wait_ge(x_lo, u)
                    for k in range(KT):
                        last = nc.tensor.transpose(XT()[:, P * k:P * (k + 1)], xt[i][:, P * k:P * (k + 1)], ident[:])
                    last.then_inc(x_turned, 1)

                def output(u, b, m):
                    pe.wait_ge(p_lo, u + 1)
                    if not isinstance(u, int) or u >= 1:
                        pe.wait_ge(out_done, 2 * u)
                    for k in range(KT):
                        if m == 0:
                            pe.wait_ge(b_loo if k % 2 else b_loe, KT // 2 * b + k // 2 + 1)
                        for n in range(2):
                            last = three(nc, O(n), [pT[x][:, k] for x in (0, 1)],
                                         [B[x][:, k, HALF * n:HALF * (n + 1)] for x in (0, 1)], k == 0, k == KT - 1)
                            if k == KT - 1:
                                last.then_inc(o_done, 1)
                        if m == M - 1 and k < KT - 1:
                            last.then_inc(b_free, 1)

                def slot(b, m, last_batch):
                    u = M * b + m
                    pe.wait_ge(x_lo, u + 1)
                    if after(b, m, 1):
                        pe.wait_ge(s_read, u)
                    for k in range(KT):
                        if m == 0:
                            pe.wait_ge(a_loo if k % 2 else a_loe, KT // 2 * b + k // 2 + 1)
                        for n in range(2):
                            last = three(nc, S()[:, HALF * n:HALF * (n + 1)], [xT[x][:, k] for x in (0, 1)],
                                         [A[x][:, k, HALF * n:HALF * (n + 1)] for x in (0, 1)], k == 0, k == KT - 1)
                        if m == M - 1 and k < KT - 1:
                            last.then_inc(a_free, 1)
                    last.then_inc(scores, 1)
                    if not (last_batch and m == M - 1):
                        turn_x(b, m + 1)
                    if after(b, m, 1):
                        if m:
                            output(u - 1, b, m - 1)
                        else:
                            output(u - 1, b - 1, M - 1)
                    pe.wait_ge(probs, u + 1)
                    if after(b, m, 1):
                        pe.wait_ge(p_lo, u)
                    for k in range(KT):
                        last = nc.tensor.transpose(PT()[:, P * k:P * (k + 1)],
                                                   pr[:, 2 * k:2 * k + 2, :].rearrange("p h s -> p (h s)"), ident[:])
                    last.then_inc(p_turned, 1)

                turn_x(0, 0)
                batches(pe, slot)
                output(NTILE - 1, BATCH - 1, M - 1)

            @block.scalar
            def _(act):
                def split_x(u):
                    act.wait_ge(x_turned, u + 1)
                    nc.scalar.copy(xT[0][:].rearrange("p k c -> p (k c)"), XT()).then_inc(x_hi, 1)

                act.wait_ge(c_loaded, 32)
                nc.scalar.activation(gt[:], gate[:], ACT.Tanh).then_inc(gated, 1)
                split_x(0)
                for c in range(2 * KT):
                    hi(act, A if c < KT else B, c, 0, True)

                def slot(b, m, last):
                    u = M * b + m
                    if not (last and m == M - 1):
                        if m == M - 1:
                            for c in range(3):
                                hi(act, A, c, b + 1, False)
                        split_x(u + 1)
                    act.wait_ge(centered, u + 1)
                    e = pr[:].rearrange("p h s -> p (h s)")
                    nc.scalar.activation(e, e, ACT.Exp).then_inc(exped, 1)
                    if m == M - 1 and not last:
                        for c in range(3, KT):
                            hi(act, A, c, b + 1, False)
                    act.wait_ge(p_turned, u + 1)
                    if after(b, m, 1):
                        act.wait_ge(o_done, 2 * u)
                    nc.scalar.copy(pT[0][:].rearrange("p k c -> p (k c)"), PT()).then_inc(p_hi, 1)
                    if m == 0 and (not isinstance(b, int) or b):
                        for c in range(KT, 2 * KT):
                            hi(act, B, c, b, False)

                batches(act, slot)

            @block.vector
            def _(dve):
                nc.vector.memset(bias[:], float("-inf")).then_inc(set_, 1)
                nc.vector.memset(zero[:], 0.0).then_inc(set_, 1)
                dve.wait_ge(set_, 2)
                dve.wait_ge(c_loaded, 32)
                nc.vector.copy_predicated(bias[:], km[:], zero[:]).then_inc(masked, 1)
                dve.wait_ge(masked, 1)
                dve.wait_ge(gated, 1)

                def split_x(u):
                    dve.wait_ge(x_hi, u + 1)
                    nc.vector.tensor_tensor(xT[1][:].rearrange("p k c -> p (k c)"), XT(),
                                            f32(xT[0][:]).rearrange("p k c -> p (k c)"), ALU.subtract)\
                        .then_inc(x_lo, 1)

                def finish(u, i):
                    for n in range(2):
                        dve.wait_ge(o_done, 2 * u + n + 1)
                        cols = slice(HALF * n, HALF * (n + 1))
                        nc.vector.scalar_tensor_tensor(out=xt[i][:, cols], in0=O(n), scalar=gt[:], in1=xt[i][:, cols],
                                                       op0=ALU.mult, op1=ALU.add).then_inc(out_done, 1)

                split_x(0)
                for c in range(1, 2 * KT, 2):
                    lo(dve, nc.vector.tensor_tensor, A if c < KT else B, c, 0)

                def slot(b, m, last):
                    u = M * b + m
                    dve.wait_ge(scores, u + 1)
                    if after(b, m, 1):
                        dve.wait_ge(p_turned, u)
                    nc.vector.scalar_tensor_tensor(out=pr[:], in0=S().rearrange("p (h s) -> p h s", h=H1), scalar=SCALE1,
                                                   in1=bias[:, bass.ds(b, 1), :].to_broadcast([P, H1, KEYS]),
                                                   op0=ALU.mult, op1=ALU.add).then_inc(s_read, 1)
                    dve.wait_ge(s_read, u + 1)
                    nc.vector.tensor_reduce(mx[:], pr[:], AX_X, ALU.max).then_inc(maxed, 1)
                    if not (last and m == M - 1):
                        split_x(u + 1)
                        if m == M - 1:
                            lo(dve, nc.vector.tensor_tensor, A, 1, b + 1)
                    dve.wait_ge(exped, u + 1)
                    nc.vector.tensor_reduce(sm[:], pr[:], AX_X, ALU.add).then_inc(summed, 1)
                    dve.wait_ge(summed, u + 1)
                    nc.vector.reciprocal(rs[:], sm[:]).then_inc(recips, 1)
                    if m == M - 1 and not last:
                        for c in range(3, KT, 2):
                            lo(dve, nc.vector.tensor_tensor, A, c, b + 1)
                    if after(b, m, 1):
                        finish(u - 1, (m - 1) % 4)
                    dve.wait_ge(p_hi, u + 1)
                    nc.vector.tensor_tensor(pT[1][:].rearrange("p k c -> p (k c)"), PT(),
                                            f32(pT[0][:]).rearrange("p k c -> p (k c)"), ALU.subtract)\
                        .then_inc(p_lo, 1)
                    if m == 0 and (not isinstance(b, int) or b):
                        for c in range(KT + 1, 2 * KT, 2):
                            lo(dve, nc.vector.tensor_tensor, B, c, b)

                batches(dve, slot)
                finish(NTILE - 1, (NTILE - 1) % 4)

            @block.gpsimd
            def _(pool):
                for c in range(0, 2 * KT, 2):
                    lo(pool, nc.gpsimd.tensor_tensor, A if c < KT else B, c, 0)

                def slot(b, m, last):
                    u = M * b + m
                    pool.wait_ge(maxed, u + 1)
                    nc.gpsimd.tensor_tensor(pr[:], pr[:], mx[:].unsqueeze(2).to_broadcast([P, H1, KEYS]),
                                            ALU.subtract).then_inc(centered, 1)
                    if m == M - 1 and not last:
                        for c in (0, 2):
                            lo(pool, nc.gpsimd.tensor_tensor, A, c, b + 1)
                    pool.wait_ge(recips, u + 1)
                    nc.gpsimd.tensor_tensor(pr[:], pr[:], rs[:].unsqueeze(2).to_broadcast([P, H1, KEYS]),
                                            ALU.mult).then_inc(probs, 1)
                    if m == M - 1 and not last:
                        for c in (4, 6):
                            lo(pool, nc.gpsimd.tensor_tensor, A, c, b + 1)
                    if m == 0 and (not isinstance(b, int) or b):
                        for c in range(KT, 2 * KT, 2):
                            lo(pool, nc.gpsimd.tensor_tensor, B, c, b)

                batches(pool, slot)


def build(nc, i, out):
    q_d = nc.dram_tensor("q_scratch", [NBLK, KT, P, BLK], F32).ap()
    x2_d = nc.dram_tensor("x2_scratch", [TOKENS, D], F32).ap()
    kbd_d = nc.dram_tensor("kbd_scratch", [BATCH, KVH0, P, 2 * GRP * KEYS], F32).ap()
    vbd_d = nc.dram_tensor("vbd_scratch", [BATCH, KVH0, P, 4 * P], F32).ap()
    a_d = nc.dram_tensor("a_scratch", [BATCH, D, D], F32).ap()
    b_d = nc.dram_tensor("b_scratch", [BATCH, D, D], F32).ap()
    x_d = i["x"].rearrange("b s d -> (b s) d")
    ctx_d = i["ctx_2048"].rearrange("b s d -> (b s) d")
    mask_d = i["mask_Bx1xSxS2_ff0"].rearrange("b o s k -> (b o s) k")
    w = {"Wk1": i["L1_xattn_Wk"], "Wv1": i["L1_xattn_Wv"], "Wq1": i["L1_xattn_Wq"], "Wo1": i["L1_xattn_Wo"],
         "gamma1": i["L1_xattn_ln_gamma"], "beta1": i["L1_xattn_ln_beta"]}
    for n in ("Wq", "Wk", "Wv", "Wo", "bq", "bk", "bv", "bo", "gamma", "beta"):
        w[n + "0"] = i["L0_xattn_" + n]
    with ExitStack() as mem:
        ident = mem.enter_context(nc.sbuf_tensor("ident", [P, P], F32))
        ps = mem.enter_context(nc.psum_tensor("ps", [P, 8 * HALF], F32))
        with ExitStack() as tables:
            normT = [tables.enter_context(nc.sbuf_tensor(f"normT{x}", [P, KT, CTX], F32R)) for x in "hl"]
            context_tables(nc, ps, ident, normT, ctx_d, w, kbd_d, vbd_d)
            layer1_tables(nc, ps, ident, normT, w, a_d, b_d)
        q_projection(nc, ps, ident, x_d, w, q_d)
        layer0(nc, ps, ident, x_d, q_d, mask_d, kbd_d, vbd_d, w, x2_d)
        layer1(nc, ps, ident, x2_d, i["mask_BxS2_bf1"], i["L1_xattn_gate"], a_d, b_d,
               out.rearrange("b s d -> (b s) d"))


_INS = ['x', 'ctx_2048', 'mask_Bx1xSxS2_ff0', 'mask_BxS2_bf1', 'L0_xattn_Wq', 'L0_xattn_bq', 'L0_xattn_Wk',
        'L0_xattn_bk', 'L0_xattn_Wv', 'L0_xattn_bv', 'L0_xattn_Wo', 'L0_xattn_bo', 'L0_xattn_gamma', 'L0_xattn_beta',
        'L1_xattn_Wq', 'L1_xattn_Wk', 'L1_xattn_Wv', 'L1_xattn_Wo', 'L1_xattn_ln_gamma', 'L1_xattn_ln_beta',
        'L1_xattn_gate']


def kernel(**inputs):
    import numpy as _np
    import concourse.bacc as _bacc
    from concourse import mybir as _mybir
    from concourse.bass_utils import run_bass_kernel_spmd as _run

    nc = _bacc.Bacc("TRN2", target_bir_lowering=False, num_devices=1)
    arrays, args = {}, {}
    for name in _INS:
        a = _np.ascontiguousarray(inputs[name])
        arrays[f"in_{name}_dram"] = a
        args[name] = nc.dram_tensor(f"in_{name}_dram", a.shape, _mybir.dt.from_np(a.dtype), kind="ExternalInput").ap()
    out = nc.dram_tensor("out_0_dram", (BATCH, SEQ, D), F32, kind="ExternalOutput").ap()
    build(nc, args, out)
    r = _run(nc, [arrays], core_ids=[0])
    return r.results[0]["out_0_dram"]
```

```python
from contextlib import ExitStack

import concourse.bass as bass
from concourse import mybir

F32 = mybir.dt.float32
F32R = mybir.dt.float32r
U8 = mybir.dt.uint8
ALU = mybir.AluOpType
ACT = mybir.ActivationFunctionType
AX_X = mybir.AxisListType.X

P = 128
BATCH, SEQ, D = 4, 1024, 1024
KEYS = 64
TOKENS = BATCH * SEQ
KT = D // P
BLK = 512
NBLK = TOKENS // BLK
TPB = BLK // P
NTILE = TOKENS // P
HALF = 512
H0, KVH0 = 32, 8
HD0 = D // H0
GRP = H0 // KVH0
KV0 = KVH0 * HD0
H1 = 16
HD1 = D // H1
SCALE0 = float(HD0) ** -0.5
SCALE1 = float(HD1) ** -0.5
EPS0, EPS1 = 1e-6, 1e-5
CTX = BATCH * KEYS


def f32(ap):
    return ap.bitcast(F32)


def three(nc, out, a, b, start, stop):
    nc.tensor.matmul(out, a[1], b[0], start=start, stop=False)
    nc.tensor.matmul(out, a[0], b[1], start=False, stop=False)
    return nc.tensor.matmul(out, a[0], b[0], start=False, stop=stop)


def row(ap, n):
    return ap.rearrange("(o n) -> o n", o=1).to_broadcast([P, n])


def context_tables(nc, ps, ident, normT, ctx_d, w, kbd_d, vbd_d):
    with ExitStack() as mem:
        def sb(name, shape, dt=F32):
            return mem.enter_context(nc.sbuf_tensor(name, shape, dt))

        def sem(name):
            return mem.enter_context(nc.semaphore(name))

        ctx = sb("ctx", [P, 2, D])
        ctxn = sb("ctxn", [P, 2, D])
        ctxT = [sb(f"ctxT{x}", [P, KT, CTX], F32R) for x in "hl"]
        wkv0 = [sb(f"wkv0{i}", [P, KT, KV0]) for i in range(2)]
        wk0 = [sb(f"wk0{x}", [P, KT, KV0], F32R) for x in "hl"]
        wv0 = [sb(f"wv0{x}", [P, KT, KV0], F32R) for x in "hl"]
        wk4 = [[sb(f"wk4{x}{i}", [P, KT, P], F32R) for x in "hl"] for i in range(2)]
        ctx2 = [[sb(f"ctx2{x}{i}", [P, KT, P], F32R) for x in "hl"] for i in range(2)]
        bk4 = sb("bk4", [P, KVH0])
        bv = sb("bv", [P, KV0])
        gam = sb("gam1", [P, D])
        bet = sb("bet1", [P, D])
        kbd = [sb(f"kbd{i}", [P, BATCH, 2, GRP, KEYS], F32R) for i in range(2)]
        vf = sb("vf", [P, KV0])
        vbd = [sb(f"vbd{i}", [P, KVH0, 2, 2, P], F32R) for i in range(2)]
        st = sb("ctx_st", [P, 2, 2, 6])
        mv = sb("ctx_mv", [P, 2, 2])
        rstd = sb("ctx_rstd", [P, 2, 1])
        nbias = sb("ctx_nbias", [P, 2, 1])
        mhalf = sb("mhalf", [P, 1])

        ctx_loaded, loaded, wloaded = sem("c_ctx_loaded"), sem("c_loaded"), sem("c_wloaded")
        zeroed = sem("c_zeroed")
        ctx_t, ctx_hi, ctx_lo = sem("c_ctx_t"), sem("c_ctx_hi"), sem("c_ctx_lo")
        stats, aggr, coef, applied, scaled, normed = (sem("c_" + n) for n in
                                                      ("stats", "aggr", "coef", "applied", "scaled", "normed"))
        wk_hi, wk_lo, w4_hi, w4_lo = sem("c_wk_hi"), sem("c_wk_lo"), sem("c_w4_hi"), sem("c_w4_lo")
        c2_hi, c2_lo = sem("c_c2_hi"), sem("c_c2_lo")
        k_done, kb_hi, kb_lo = sem("c_k_done"), sem("c_kb_hi"), sem("c_kb_lo")
        kb_out = [sem(f"c_kb_out{i}") for i in range(2)]
        v_done, v_copied, vb_hi, vb_lo = (sem("c_" + n) for n in ("v_done", "v_copied", "vb_hi", "vb_lo"))
        vb_out = [sem(f"c_vb_out{i}") for i in range(2)]

        with nc.Block() as block:
            @block.sync
            def _(sp):
                sp.dma_start(ctx[:], ctx_d.rearrange("(r p) d -> p r d", p=P)).then_inc(ctx_loaded, 16)
                sp.dma_start(wkv0[0][:], w["Wk0"].rearrange("(k p) n -> p k n", p=P)).then_inc(wloaded, 16)
                sp.dma_start(wkv0[1][:], w["Wv0"].rearrange("(k p) n -> p k n", p=P)).then_inc(wloaded, 16)
                for j in range(GRP):
                    sp.dma_start(bk4[HD0 * j:HD0 * (j + 1), :],
                                 w["bk0"].rearrange("(g d) -> d g", d=HD0), allow_slow_non_contiguous=True)\
                        .then_inc(loaded, 16)
                sp.dma_start(bv[:], row(w["bv0"], KV0)).then_inc(loaded, 16)
                sp.dma_start(gam[:], row(w["gamma1"], D)).then_inc(loaded, 16)
                sp.dma_start(bet[:], row(w["beta1"], D)).then_inc(loaded, 16)
                for g in range(KVH0):
                    sp.wait_ge(kb_hi, g + 1)
                    sp.wait_ge(kb_lo, g + 1)
                    sp.dma_start(kbd_d[:, g].rearrange("b p c -> p b c"),
                                 f32(kbd[g % 2][:]).rearrange("p b x j s -> p b (x j s)")).then_inc(kb_out[g % 2], 16)
                for b in range(BATCH):
                    sp.wait_ge(vb_hi, b + 1)
                    sp.wait_ge(vb_lo, b + 1)
                    sp.dma_start(vbd_d[b].rearrange("g p c -> p g c"),
                                 f32(vbd[b % 2][:]).rearrange("p g x u c -> p g (x u c)"))\
                        .then_inc(vb_out[b % 2], 16)
                for i in range(2):
                    sp.wait_ge(kb_out[i], 16 * KVH0 // 2)
                for i in range(2):
                    sp.wait_ge(vb_out[i], 16 * BATCH // 2)

            @block.gpsimd
            def _(pool):
                nc.gpsimd.memset(ident[:], 0.0).then_inc(zeroed, 1)
                pool.wait_ge(zeroed, 1)
                nc.gpsimd.affine_select(out=ident[:], in_=ident[:], compare_op=ALU.not_equal, fill=1.0, base=0,
                                        pattern=[[-1, P]], channel_multiplier=1).then_inc(zeroed, 1)
                nc.gpsimd.memset(mhalf[:], -0.5).then_inc(zeroed, 1)
                for i in range(2):
                    nc.gpsimd.memset(f32(kbd[i][:]), 0.0).then_inc(zeroed, 1)
                for i in range(2):
                    nc.gpsimd.memset(f32(vbd[i][:]), 0.0).then_inc(zeroed, 1)
                pool.wait_ge(zeroed, 3)
                pool.wait_ge(aggr, 2)
                nc.gpsimd.tensor_scalar(rstd[:], mv[:, :, 1:2], EPS1, None, ALU.add).then_inc(coef, 1)
                pool.wait_ge(coef, 1)
                for r in range(2):
                    nc.gpsimd.tensor_tensor(rstd[:, r], rstd[:, r], mhalf[:], ALU.pow).then_inc(coef, 1)
                pool.wait_ge(coef, 3)
                for r in range(2):
                    nc.gpsimd.tensor_scalar(nbias[:, r], mv[:, r, 0:1], rstd[:, r], -1.0, ALU.mult,
                                            ALU.mult).then_inc(coef, 1)
                for r in range(2):
                    pool.wait_ge(scaled, r + 1)
                    nc.gpsimd.tensor_tensor(ctxn[:, r], ctxn[:, r], bet[:], ALU.add).then_inc(normed, 1)

            def key_hi(act, g):
                act.wait_ge(k_done, g + 1)
                act.wait_ge(loaded, 16 * 7)
                act.wait_ge(zeroed, 5)
                if g >= 2:
                    act.wait_ge(kb_out[g % 2], 16 * (g // 2))
                for j in range(GRP):
                    r = slice(HD0 * j, HD0 * (j + 1))
                    last = nc.scalar.activation(kbd[g % 2][r, :, 0, j, :], ps[r, 2048 + HALF * (g % 2):][:, :CTX]
                                                .rearrange("p (b s) -> p b s", b=BATCH), ACT.Identity,
                                                bias=bk4[r, g:g + 1])
                last.then_inc(kb_hi, 1)

            def val_hi(act, b):
                act.wait_ge(v_copied, b + 1)
                act.wait_ge(zeroed, 7)
                if b >= 2:
                    act.wait_ge(vb_out[b % 2], 16 * (b // 2))
                for i in range(2):
                    r = slice(KEYS * i, KEYS * (i + 1))
                    for u in range(2):
                        c = HD0 * (2 * u + i)
                        last = nc.scalar.copy(vbd[b % 2][r, :, 0, u, c:c + HD0], vf[r, :].rearrange("p (g d) -> p g d", g=KVH0))
                last.then_inc(vb_hi, 1)

            @block.scalar
            def _(act):
                act.wait_ge(ctx_t, 1)
                for i in range(4):
                    nc.scalar.copy(ctxT[0][:, 2 * i:2 * i + 2, :], ps[:, HALF * i:HALF * (i + 1)]).then_inc(ctx_hi, 1)
                act.wait_ge(wloaded, 32)
                nc.scalar.copy(wk0[0][:], wkv0[0][:]).then_inc(wk_hi, 1)
                nc.scalar.copy(wv0[0][:], wkv0[1][:]).then_inc(wk_hi, 1)
                act.wait_ge(wk_hi, 1)
                for g in range(KVH0):
                    if g >= 2:
                        act.wait_ge(k_done, g - 1)
                    for j in range(GRP):
                        last = nc.scalar.copy(wk4[g % 2][0][:, :, HD0 * j:HD0 * (j + 1)],
                                              wkv0[0][:, :, HD0 * g:HD0 * (g + 1)])
                    last.then_inc(w4_hi, 1)
                    if g == 1:
                        act.wait_ge(coef, 5)
                        for r in range(2):
                            nc.scalar.activation(ctxn[:, r], ctx[:, r], ACT.Identity, scale=rstd[:, r],
                                                 bias=nbias[:, r]).then_inc(applied, 1)
                    if g >= 1:
                        key_hi(act, g - 1)
                    if g == 4:
                        act.wait_ge(ctx_t, 2)
                        for i in range(4):
                            nc.scalar.copy(normT[0][:, 2 * i:2 * i + 2, :], ps[:, HALF * i:HALF * (i + 1)]).then_inc(ctx_hi, 1)
                key_hi(act, KVH0 - 1)
                for b in range(BATCH):
                    if b >= 2:
                        act.wait_ge(v_done, b - 1)
                    for i in range(2):
                        last = nc.scalar.copy(ctx2[b % 2][0][:, :, KEYS * i:KEYS * (i + 1)],
                                              f32(ctxT[0][:, :, KEYS * b:KEYS * (b + 1)]))
                    last.then_inc(c2_hi, 1)
                    if b >= 1:
                        val_hi(act, b - 1)
                val_hi(act, BATCH - 1)

            @block.vector
            def _(dve):
                dve.wait_ge(ctx_loaded, 16)
                for r in range(2):
                    for n in range(2):
                        nc.vector.bn_stats(st[:, r, n], ctx[:, r, HALF * n:HALF * (n + 1)]).then_inc(stats, 1)
                dve.wait_ge(stats, 4)
                for r in range(2):
                    nc.vector.bn_aggr(mv[:, r], st[:, r]).then_inc(aggr, 1)
                for i in range(4):
                    dve.wait_ge(ctx_hi, i + 1)
                    nc.vector.tensor_tensor(ctxT[1][:, 2 * i:2 * i + 2, :], ps[:, HALF * i:HALF * (i + 1)]
                                            .rearrange("p (k c) -> p k c", k=2),
                                            f32(ctxT[0][:, 2 * i:2 * i + 2, :]), ALU.subtract).then_inc(ctx_lo, 1)
                for i, (h, l) in enumerate((wk0, wv0)):
                    dve.wait_ge(wk_hi, i + 1)
                    nc.vector.tensor_tensor(l[:], wkv0[i][:], f32(h[:]), ALU.subtract).then_inc(wk_lo, 1)
                dve.wait_ge(wk_lo, 1)

                def key_lo(g):
                    dve.wait_ge(kb_hi, g + 1)
                    for j in range(GRP):
                        r = slice(HD0 * j, HD0 * (j + 1))
                        last = nc.vector.scalar_tensor_tensor(
                            out=kbd[g % 2][r, :, 1, j, :], in0=ps[r, 2048 + HALF * (g % 2):][:, :CTX]
                            .rearrange("p (b s) -> p b s", b=BATCH), scalar=bk4[r, g:g + 1],
                            in1=f32(kbd[g % 2][r, :, 0, j, :]), op0=ALU.add, op1=ALU.subtract)
                    last.then_inc(kb_lo, 1)

                for g in range(KVH0):
                    if g >= 2:
                        dve.wait_ge(k_done, g - 1)
                    for j in range(GRP):
                        last = nc.vector.tensor_copy(wk4[g % 2][1][:, :, HD0 * j:HD0 * (j + 1)],
                                                     f32(wk0[1][:, :, HD0 * g:HD0 * (g + 1)]))
                    last.then_inc(w4_lo, 1)
                    if g >= 1:
                        key_lo(g - 1)
                    if g == 1:
                        dve.wait_ge(loaded, 16 * 7)
                        for r in range(2):
                            dve.wait_ge(applied, r + 1)
                            nc.vector.tensor_tensor(ctxn[:, r], ctxn[:, r], gam[:], ALU.mult).then_inc(scaled, 1)
                    if g == 4:
                        for i in range(4):
                            dve.wait_ge(ctx_hi, 5 + i)
                            nc.vector.tensor_tensor(normT[1][:, 2 * i:2 * i + 2, :], ps[:, HALF * i:HALF * (i + 1)]
                                                    .rearrange("p (k c) -> p k c", k=2),
                                                    f32(normT[0][:, 2 * i:2 * i + 2, :]), ALU.subtract).then_inc(ctx_lo, 1)
                key_lo(KVH0 - 1)

                def val_lo(b):
                    dve.wait_ge(v_done, b + 1)
                    if b >= 1:
                        dve.wait_ge(vb_hi, b)
                        dve.wait_ge(vb_lo, b)
                    nc.vector.tensor_tensor(vf[:], ps[:, 3072 + HALF * (b % 2):][:, :KV0], bv[:], ALU.add)\
                        .then_inc(v_copied, 1)
                    dve.wait_ge(vb_hi, b + 1)
                    dve.wait_ge(v_copied, b + 1)
                    for i in range(2):
                        r = slice(KEYS * i, KEYS * (i + 1))
                        for u in range(2):
                            c = HD0 * (2 * u + i)
                            last = nc.vector.tensor_tensor(
                                vbd[b % 2][r, :, 1, u, c:c + HD0], vf[r, :].rearrange("p (g d) -> p g d", g=KVH0),
                                f32(vbd[b % 2][r, :, 0, u, c:c + HD0]), ALU.subtract)
                    last.then_inc(vb_lo, 1)

                for b in range(BATCH):
                    if b >= 2:
                        dve.wait_ge(v_done, b - 1)
                    for i in range(2):
                        last = nc.vector.tensor_copy(ctx2[b % 2][1][:, :, KEYS * i:KEYS * (i + 1)],
                                                     f32(ctxT[1][:, :, KEYS * b:KEYS * (b + 1)]))
                    last.then_inc(c2_lo, 1)
                    if b >= 1:
                        val_lo(b - 1)
                val_lo(BATCH - 1)

            @block.tensor
            def _(pe):
                def turn(src):
                    for k in range(KT):
                        for r in range(2):
                            last = nc.tensor.transpose(ps[:, CTX * k + P * r:][:, :P], src[:, r, P * k:P * (k + 1)],
                                                       ident[:])
                    last.then_inc(ctx_t, 1)

                pe.wait_ge(zeroed, 2)
                pe.wait_ge(ctx_loaded, 16)
                turn(ctx)
                pe.wait_ge(ctx_lo, 4)
                for g in range(KVH0):
                    if g == 3:
                        pe.wait_ge(normed, 2)
                        turn(ctxn)
                    pe.wait_ge(w4_hi, g + 1)
                    pe.wait_ge(w4_lo, g + 1)
                    if g >= 2:
                        pe.wait_ge(kb_lo, g - 1)
                    for k in range(KT):
                        last = three(nc, ps[:, 2048 + HALF * (g % 2):][:, :CTX], [wk4[g % 2][x][:, k] for x in (0, 1)],
                                     [ctxT[x][:, k] for x in (0, 1)], k == 0, k == KT - 1)
                    last.then_inc(k_done, 1)
                pe.wait_ge(wk_lo, 2)
                for b in range(BATCH):
                    pe.wait_ge(c2_hi, b + 1)
                    pe.wait_ge(c2_lo, b + 1)
                    if b >= 2:
                        pe.wait_ge(v_copied, b - 1)
                    for k in range(KT):
                        last = three(nc, ps[:, 3072 + HALF * (b % 2):][:, :KV0], [ctx2[b % 2][x][:, k] for x in (0, 1)],
                                     [(wv0[x])[:, k] for x in (0, 1)], k == 0, k == KT - 1)
                    last.then_inc(v_done, 1)


def layer1_tables(nc, ps, ident, normT, w, a_d, b_d):
    with ExitStack() as mem:
        def sb(name, shape, dt=F32):
            return mem.enter_context(nc.sbuf_tensor(name, shape, dt))

        def sem(name):
            return mem.enter_context(nc.semaphore(name))

        KV = range(2)
        wt = [sb(f"wt{i}", [P, D]) for i in KV]
        wq = sb("wq1", [P, D])
        wo = sb("wo1", [P, KT, P])
        wT = [[sb(f"wT{i}{x}", [P, KT, P], F32R) for x in "hl"] for i in KV]
        wqs = [sb(f"wqs{x}", [P, D], F32R) for x in "hl"]
        woT = [sb(f"woT{x}", [P, D], F32R) for x in "hl"]
        bd = [[sb(f"bd{i}{x}", [P, BATCH, 2, KEYS], F32R) for x in "hl"] for i in KV]
        ost = [sb(f"ost{i}", [P, HALF]) for i in range(8)]
        names = ("zeroed wt_loaded wq_loaded wo_loaded turned wT_hi wT_lo wo_turned wo_hi wo_lo wq_hi wq_lo "
                 "proj bd_hi bd_lo outer evac_a evac_d").split()
        s = {n: sem("l_" + n) for n in names}
        stored = [sem(f"l_stored{i}") for i in range(8)]

        with nc.Block() as block:
            @block.sync
            def _(sp):
                def load(f, later):
                    if later:
                        sp.wait_ge(s["turned"], 2 * f)
                    sp.dma_start(wt[0][:], w["Wk1"][bass.ds(f * P, P), :]).then_inc(s["wt_loaded"], 16)
                    sp.dma_start(wt[1][:], w["Wv1"][bass.ds(f * P, P), :]).then_inc(s["wt_loaded"], 16)
                    if later:
                        sp.wait_ge(s["wq_lo"], f)
                        sp.wait_ge(s["wo_turned"], f)
                    sp.dma_start(wq[:], w["Wq1"][bass.ds(f * P, P), :]).then_inc(s["wq_loaded"], 16)
                    sp.dma_start(wo[:], w["Wo1"].rearrange("(o p) c -> p o c", p=P)[:, :, bass.ds(f * P, P)])\
                        .then_inc(s["wo_loaded"], 16)

                def store(f):
                    for o in range(16):
                        i, e = divmod(o, 8)
                        sp.wait_ge(s["evac_d" if o % 2 else "evac_a"], 8 * f + o // 2 + 1)
                        if i == 0:
                            dst = a_d[:, P * e:P * (e + 1), :][:, :, bass.ds(f * P, P)].rearrange("b p c -> p b c")
                            src = ost[o % 8][:].rearrange("p (b c) -> p b c", b=BATCH)
                        else:
                            b, n = divmod(e, 2)
                            dst = b_d[b][bass.ds(f * P, P), :][:, HALF * n:HALF * (n + 1)]
                            src = ost[o % 8][:]
                        sp.dma_start(dst, src).then_inc(stored[o % 8], 16)

                load(0, False)
                with sp.Fori(0, KT - 1) as f:
                    load(f + 1, True)
                    store(f)
                store(KT - 1)
                for i in range(8):
                    sp.wait_ge(stored[i], 16 * 2 * KT)

            def evacuate(eng, copy, odd, f, done):
                for o in range(odd, 16, 2):
                    eng.wait_ge(s["outer"], 16 * f + o + 1)
                    if not isinstance(f, int) or o >= 8:
                        eng.wait_ge(stored[o % 8], 16 * (2 * f + o // 8))
                    copy(ost[o % 8][:], ps[:, 3072 + HALF * (o % 2):][:, :HALF]).then_inc(done, 1)

            def act_pair(act, f):
                for i in KV:
                    act.wait_ge(s["turned"], 2 * f + i + 1)
                    if not isinstance(f, int) or f:
                        act.wait_ge(s["proj"], 2 * (f - 1) + i + 1)
                    nc.scalar.copy(wT[i][0][:], ps[:, D * i:D * (i + 1)]).then_inc(s["wT_hi"], 1)
                act.wait_ge(s["wq_loaded"], 16 * (f + 1))
                if not isinstance(f, int) or f:
                    act.wait_ge(s["outer"], 16 * f)
                nc.scalar.copy(wqs[0][:], wq[:]).then_inc(s["wq_hi"], 1)
                act.wait_ge(s["wo_turned"], f + 1)
                nc.scalar.copy(woT[0][:], ps[:, 0:D]).then_inc(s["wo_hi"], 1)
                act.wait_ge(s["zeroed"], 4)
                for i in KV:
                    act.wait_ge(s["proj"], 2 * f + i + 1)
                    for h in range(2):
                        r = slice(HD1 * h, HD1 * (h + 1))
                        last = nc.scalar.copy(bd[i][0][r, :, h, :], ps[r, 2048 + HALF * i:][:, :CTX]
                                              .rearrange("p (b s) -> p b s", b=BATCH))
                    last.then_inc(s["bd_hi"], 1)
                evacuate(act, nc.scalar.copy, 0, f, s["evac_a"])

            @block.scalar
            def _(act):
                act_pair(act, 0)
                with act.Fori(1, KT) as f:
                    act_pair(act, f)

            def dve_pair(dve, f):
                for i in KV:
                    dve.wait_ge(s["wT_hi"], 2 * f + i + 1)
                    nc.vector.tensor_tensor(wT[i][1][:], ps[:, D * i:D * (i + 1)].rearrange("p (k c) -> p k c", k=KT),
                                            f32(wT[i][0][:]), ALU.subtract).then_inc(s["wT_lo"], 1)
                dve.wait_ge(s["wo_hi"], f + 1)
                nc.vector.tensor_tensor(woT[1][:], ps[:, 0:D], f32(woT[0][:]), ALU.subtract).then_inc(s["wo_lo"], 1)
                for i in KV:
                    dve.wait_ge(s["bd_hi"], 2 * f + i + 1)
                    for h in range(2):
                        r = slice(HD1 * h, HD1 * (h + 1))
                        last = nc.vector.tensor_tensor(bd[i][1][r, :, h, :], ps[r, 2048 + HALF * i:][:, :CTX]
                                                       .rearrange("p (b s) -> p b s", b=BATCH),
                                                       f32(bd[i][0][r, :, h, :]), ALU.subtract)
                    last.then_inc(s["bd_lo"], 1)
                evacuate(dve, nc.vector.tensor_copy, 1, f, s["evac_d"])

            @block.vector
            def _(dve):
                dve_pair(dve, 0)
                with dve.Fori(1, KT) as f:
                    dve_pair(dve, f)

            @block.gpsimd
            def _(pool):
                for i in KV:
                    for x in range(2):
                        nc.gpsimd.memset(f32(bd[i][x][:]), 0.0).then_inc(s["zeroed"], 1)
                with pool.Fori(0, KT) as f:
                    pool.wait_ge(s["wq_hi"], f + 1)
                    nc.gpsimd.tensor_tensor(wqs[1][:], wq[:], f32(wqs[0][:]), ALU.subtract).then_inc(s["wq_lo"], 1)

            def pe_pair(pe, f):
                later = not isinstance(f, int) or f > 0
                for i in KV:
                    pe.wait_ge(s["wt_loaded"], 16 * (2 * f + 2))
                    if later and i == 0:
                        pe.wait_ge(s["wo_lo"], f)
                    for k in range(KT):
                        last = nc.tensor.transpose(ps[:, D * i + P * k:][:, :P], wt[i][:, P * k:P * (k + 1)], ident[:])
                    last.then_inc(s["turned"], 1)

                def project(i):
                    pe.wait_ge(s["wT_lo"], 2 * f + i + 1)
                    for k in range(KT):
                        last = three(nc, ps[:, 2048 + HALF * i:][:, :CTX], [wT[i][x][:, k] for x in (0, 1)],
                                     [normT[x][:, k] for x in (0, 1)], k == 0, k == KT - 1)
                    last.then_inc(s["proj"], 1)

                project(0)
                pe.wait_ge(s["wo_loaded"], 16 * (f + 1))
                for o in range(KT):
                    last = nc.tensor.transpose(ps[:, P * o:P * (o + 1)], wo[:, o, :], ident[:])
                last.then_inc(s["wo_turned"], 1)
                project(1)
                for o in range(16):
                    i, e = divmod(o, 8)
                    if o == 0:
                        pe.wait_ge(s["bd_lo"], 2 * f + 1)
                        pe.wait_ge(s["wq_lo"], f + 1)
                    if o == 8:
                        pe.wait_ge(s["bd_lo"], 2 * f + 2)
                        pe.wait_ge(s["wo_lo"], f + 1)
                    if o >= 2 or later:
                        pe.wait_ge(s["evac_d" if o % 2 else "evac_a"], 8 * f + o // 2)
                    out = ps[:, 3072 + HALF * (o % 2):][:, :HALF]
                    if i == 0:
                        a = [wqs[x][:, P * e:P * (e + 1)] for x in (0, 1)]
                        b = [bd[0][x][:].rearrange("p b h s -> p (b h s)") for x in (0, 1)]
                    else:
                        a = [bd[1][x][:, e // 2].rearrange("p h s -> p (h s)") for x in (0, 1)]
                        b = [woT[x][:, HALF * (e % 2):HALF * (e % 2 + 1)] for x in (0, 1)]
                    three(nc, out, a, b, True, True).then_inc(s["outer"], 1)

            @block.tensor
            def _(pe):
                pe_pair(pe, 0)
                with pe.Fori(1, KT) as f:
                    pe_pair(pe, f)


def q_projection(nc, ps, ident, x_d, w, q_d):
    with ExitStack() as mem:
        def sb(name, shape, dt=F32):
            return mem.enter_context(nc.sbuf_tensor(name, shape, dt))

        def sem(name):
            return mem.enter_context(nc.semaphore("q_" + name))

        wq = [sb(f"wq0{x}", [P, KT, D], F32R) for x in "hl"]
        raw = [sb(f"wraw{i}", [P, D]) for i in range(3)]
        bq = sb("bq", [P, KT])
        xt = [sb(f"xt{i}", [P, D]) for i in range(4)]
        xT = [[sb(f"xT{i}{x}", [P, KT, BLK], F32R) for x in "hl"] for i in range(2)]
        qst = [sb(f"qst{i}", [P, BLK]) for i in range(4)]
        b_loaded, w_hi, w_lo = sem("b_loaded"), sem("w_hi"), sem("w_lo")
        turned, x_hi, x_lo = sem("turned"), sem("x_hi"), sem("x_lo")
        q_done, q_out = sem("q_done"), sem("q_out")
        w_loaded = [sem(f"w_loaded{i}") for i in range(3)]
        x_loaded = [sem(f"x_loaded{i}") for i in range(4)]
        q_stored = [sem(f"q_stored{i}") for i in range(4)]

        def pairs(eng, body):
            body(0, 0, True)
            body(1, 1, True)
            with eng.Fori(1, NBLK // 2 - 1) as i:
                body(2 * i, 0, True)
                body(2 * i + 1, 1, True)
            body(NBLK - 2, 0, True)
            body(NBLK - 1, 1, False)

        with nc.Block() as block:
            @block.sync
            def _(sp):
                def load(t, m):
                    if not isinstance(t, int) or t:
                        sp.wait_ge(turned, 4 * (t - 1) + m + 1)
                    sp.dma_start(xt[m][:], x_d[bass.ds(BLK * t + P * m, P), :]).then_inc(x_loaded[m], 16)

                for m in range(TPB):
                    load(0, m)
                for k in range(KT):
                    if k >= 3:
                        sp.wait_ge(w_lo, k - 2)
                    sp.dma_start(raw[k % 3][:], w["Wq0"][P * k:P * (k + 1), :]).then_inc(w_loaded[k % 3], 16)
                sp.dma_start(bq[:], w["bq0"].rearrange("(g p) -> p g", p=P), allow_slow_non_contiguous=True)\
                    .then_inc(b_loaded, 16)

                def body(t, par, more):
                    for g in range(KT):
                        if more and g % 2 == 0:
                            load(t + 1, g // 2)
                        sp.wait_ge(q_out, 8 * t + g + 1)
                        sp.dma_start(q_d[t, g], qst[g % 4][:]).then_inc(q_stored[g % 4], 16)

                pairs(sp, body)
                for i in range(4):
                    sp.wait_ge(q_stored[i], 16 * 2 * NBLK)

            def x_hi_part(act, t, par, m):
                act.wait_ge(turned, 4 * t + m + 1)
                nc.scalar.copy(xT[par][0][:, :, P * m:P * (m + 1)], ps[:, D * (m % 2):][:, :D]
                               .rearrange("p (k c) -> p k c", k=KT)).then_inc(x_hi, 1)

            @block.scalar
            def _(act):
                for m in range(TPB):
                    x_hi_part(act, 0, 0, m)
                    for k in (2 * m, 2 * m + 1):
                        act.wait_ge(w_loaded[k % 3], 16 * (k // 3 + 1))
                        nc.scalar.copy(wq[0][:, k], raw[k % 3][:]).then_inc(w_hi, 1)
                act.wait_ge(b_loaded, 16)

                def body(t, par, more):
                    for g in range(KT):
                        if more and g % 2 == 1:
                            x_hi_part(act, t + 1, 1 - par, g // 2)
                        act.wait_ge(q_done, 8 * t + g + 1)
                        if not isinstance(t, int) or 8 * t + g >= 4:
                            act.wait_ge(q_stored[g % 4], 16 * (2 * t + g // 4))
                        nc.scalar.activation(qst[g % 4][:], ps[:, 2048 + HALF * (g % 4):][:, :HALF], ACT.Identity,
                                             bias=bq[:, g:g + 1]).then_inc(q_out, 1)

                pairs(act, body)

            def x_lo_part(dve, t, par, m):
                dve.wait_ge(x_hi, 4 * t + m + 1)
                nc.vector.tensor_tensor(xT[par][1][:, :, P * m:P * (m + 1)], ps[:, D * (m % 2):][:, :D]
                                        .rearrange("p (k c) -> p k c", k=KT),
                                        f32(xT[par][0][:, :, P * m:P * (m + 1)]), ALU.subtract).then_inc(x_lo, 1)

            @block.vector
            def _(dve):
                for m in range(TPB):
                    x_lo_part(dve, 0, 0, m)
                    for k in (2 * m, 2 * m + 1):
                        dve.wait_ge(w_hi, k + 1)
                        nc.vector.tensor_tensor(wq[1][:, k], raw[k % 3][:], f32(wq[0][:, k]), ALU.subtract)\
                            .then_inc(w_lo, 1)

                def body(t, par, more):
                    for m in range(TPB):
                        if more:
                            x_lo_part(dve, t + 1, 1 - par, m)

                pairs(dve, body)

            @block.tensor
            def _(pe):
                def turn(t, m):
                    pe.wait_ge(x_loaded[m], 16 * (t + 1))
                    if not isinstance(t, int) or 4 * t + m >= 2:
                        pe.wait_ge(x_lo, 4 * t + m - 1)
                    for k in range(KT):
                        last = nc.tensor.transpose(ps[:, D * (m % 2) + P * k:][:, :P], xt[m][:, P * k:P * (k + 1)],
                                                   ident[:])
                    last.then_inc(turned, 1)

                for m in range(TPB):
                    turn(0, m)

                def body(t, par, more):
                    pe.wait_ge(x_lo, 4 * (t + 1))
                    for g in range(KT):
                        if more and g % 2 == 1:
                            turn(t + 1, g // 2)
                        if not isinstance(t, int) or 8 * t + g >= 4:
                            pe.wait_ge(q_out, 8 * t + g - 3)
                        for k in range(KT):
                            if isinstance(t, int) and t == 0 and g == 0:
                                pe.wait_ge(w_lo, k + 1)
                            last = three(nc, ps[:, 2048 + HALF * (g % 4):][:, :HALF],
                                         [wq[x][:, k, P * g:P * (g + 1)] for x in (0, 1)],
                                         [xT[par][x][:, k] for x in (0, 1)], k == 0, k == KT - 1)
                        last.then_inc(q_done, 1)

                pairs(pe, body)


def layer0(nc, ps, ident, x_d, q_d, mask_d, kbd_d, vbd_d, w, x2_d):
    with ExitStack() as mem:
        def sb(name, shape, dt=F32):
            return mem.enter_context(nc.sbuf_tensor(name, shape, dt))

        def sem(name):
            return mem.enter_context(nc.semaphore("a_" + name))

        wo = [sb(f"wo0{x}", [P, KT, D], F32R) for x in "hl"]
        oT = [[sb(f"oT{i}{x}", [P, KT, BLK], F32R) for x in "hl"] for i in range(2)]
        kb = [sb(f"kb{i}", [P, 2, GRP * KEYS], F32R) for i in range(2)]
        vb = [sb(f"vb{i}", [P, 2, 2, P], F32R) for i in range(2)]
        qf = [sb(f"qf{i}", [P, BLK]) for i in range(2)]
        qs = [[sb(f"qs{i}{x}", [P, BLK], F32R) for x in "hl"] for i in range(2)]
        pr = [sb(f"pr{i}", [P, TPB, GRP, KEYS]) for i in range(2)]
        pT = [sb(f"pT{x}", [P, 2, BLK], F32R) for x in "hl"]
        xb = [sb(f"xb{i}", [P, D]) for i in range(2)]
        y = [sb(f"y{i}", [P, D]) for i in range(2)]
        mask = [sb(f"mask{i}", [P, TPB, KEYS]) for i in range(2)]
        gam, bet, bo = sb("gam0", [P, D]), sb("bet0", [P, D]), sb("bo0", [P, D])
        mx, sm, rs = sb("mx", [P, TPB * GRP]), sb("sm", [P, TPB * GRP]), sb("rs", [P, TPB * GRP])
        st, mv = sb("st", [P, 2, 6]), sb("mv", [P, 2])
        rstd, nbias, mhalf = sb("rstd", [P, 1]), sb("nbias", [P, 1]), sb("mhalf0", [P, 1])
        eps, minus = sb("eps", [P, 1]), sb("minus", [P, 1])

        S, TR, V = ps[:, 0:1024], ps[:, 1024:2048], ps[:, 2048:2560]

        def O(n):
            return ps[:, 2560 + HALF * n:][:, :HALF]

        (w_hi, w_lo, c_loaded, half_set, m_loaded, q_hi, q_lo, scores, s_read, maxed, centered, exped, summed, recips,
         probs, turned, pt_hi, pt_lo, pv, o_hi, o_lo, o_done, xbo, y_done, st_done, aggr, coef, applied, scaled,
         normed) = (sem(n) for n in (
             "w_hi w_lo c_loaded half_set m_loaded q_hi q_lo scores s_read maxed centered exped summed recips probs "
             "turned pt_hi pt_lo pv o_hi o_lo o_done xbo y_done st_done aggr coef applied scaled normed").split())
        w_loaded = [sem(f"w_loaded{i}") for i in range(2)]
        q_loaded, k_loaded, v_loaded, x_loaded, stored = (
            [sem(f"{n}{i}") for i in range(2)] for n in "q_loaded k_loaded v_loaded x_loaded stored".split())

        def blocks(slot):
            def block_of(t, par):
                for g in range(KT):
                    slot(t, par, g)

            def run(eng):
                block_of(0, 0)
                block_of(1, 1)
                with eng.Fori(1, NBLK // 2 - 1) as i:
                    block_of(2 * i, 0)
                    block_of(2 * i + 1, 1)
                block_of(NBLK - 2, 0)
                block_of(NBLK - 1, 1)
                block_of(NBLK, 0)
                slot(NBLK + 1, 1, 0)
            return run

        def looped(t):
            return not isinstance(t, int)

        def after(t, g, n):
            return looped(t) or 8 * t + g >= n

        def attends(t, g, lag=0):
            return looped(t) or 0 <= 8 * t + g - lag < 8 * NBLK

        def projected(t, par, g):
            T, tp, G = (t, par, g - 1) if g else (t - 1, 1 - par, KT - 1)
            return T, tp, G, looped(t) or 1 <= T <= NBLK

        def lagging(T, G):
            if G % 2 or (not looped(T) and not 0 <= 4 * (T - 1) + G // 2 - 1 < NTILE - 1):
                return None
            return 4 * (T - 1) + G // 2 - 1

        def upcoming(T, G):
            n = 4 * (T - 1) + G // 2 + 1
            return n if looped(T) or 0 <= n < NTILE else None

        with nc.Block() as block:
            @block.sync
            def _(sp):
                def load_q(u, g):
                    sp.dma_start(qf[g % 2][:], q_d.rearrange("t g p c -> (t g) p c")[u]).then_inc(q_loaded[g % 2], 16)

                def load_k(t, g):
                    sp.dma_start(f32(kb[g % 2][:]).rearrange("p x c -> p (x c)"), kbd_d[t // 2, g])\
                        .then_inc(k_loaded[g % 2], 16)

                def load_v(t, g):
                    sp.dma_start(f32(vb[g % 2][:]).rearrange("p x u c -> p (x u c)"), vbd_d[t // 2, g])\
                        .then_inc(v_loaded[g % 2], 16)

                def load_mask(t, par):
                    sp.dma_start(mask[par][:], mask_d[bass.ds(BLK * t, BLK), :].rearrange("(m p) s -> p m s", p=P))\
                        .then_inc(m_loaded, 16)

                load_q(0, 0)
                load_k(0, 0)
                load_mask(0, 0)
                load_q(1, 1)
                load_k(0, 1)

                def slot(t, par, g):
                    u = 8 * t + g
                    T, _, G, _ = projected(t, par, g)
                    if g == 1 and (looped(t) or t < NBLK - 1):
                        sp.wait_ge(s_read, u)
                        load_mask(t + 1, 1 - par)
                    if attends(t, g, -2):
                        g2, t2 = (g + 2) % KT, t + (g + 2) // KT
                        sp.wait_ge(q_lo, u + 1)
                        load_q(u + 2, g2)
                        if after(t, g, 3):
                            sp.wait_ge(pv, u - 2)
                        sp.wait_ge(scores, u + 1)
                        load_k(t2, g2)
                    elif attends(t, g, 1):
                        sp.wait_ge(pv, u - 2)
                    if attends(t, g, 1):
                        load_v(t - (g == 0), (g - 1) % KT)
                    if not looped(t) and t == 0:
                        if g >= 2:
                            sp.wait_ge(w_lo, g - 1)
                        sp.dma_start(y[g % 2][:], w["Wo0"][P * g:P * (g + 1), :]).then_inc(w_loaded[g % 2], 16)
                        if g < 3:
                            sp.dma_start((gam, bet, bo)[g][:], row(w[("gamma0", "beta0", "bo0")[g]], D))\
                                .then_inc(c_loaded, 16)
                    n = upcoming(T, G)
                    if G % 2 == 0 and n is not None:
                        if looped(n) or n >= 2:
                            sp.wait_ge(y_done, 2 * (n - 1))
                        sp.dma_start(xb[(G // 2 + 1) % 2][:], x_d[bass.ds(P * n, P), :])\
                            .then_inc(x_loaded[(G // 2 + 1) % 2], 16)
                    if G % 2 == 1 and lagging(T, G - 1) is not None:
                        n = lagging(T, G - 1)
                        sp.wait_ge(normed, n + 1)
                        sp.dma_start(x2_d[bass.ds(P * n, P), :], y[(G // 2 + 1) % 2][:])\
                            .then_inc(stored[(G // 2 + 1) % 2], 16)

                blocks(slot)(sp)
                sp.wait_ge(normed, NTILE)
                sp.dma_start(x2_d[P * (NTILE - 1):P * NTILE, :], y[(NTILE - 1) % 2][:])\
                    .then_inc(stored[(NTILE - 1) % 2], 16)
                for i in range(2):
                    sp.wait_ge(stored[i], 16 * NTILE // 2)

            @block.tensor
            def _(pe):
                def output(T, tp, G, fs):
                    m, n = divmod(G, 2)
                    h = 8 * (T - 1) + G
                    if fs[0] == 0:
                        if looped(h) or h >= 2:
                            pe.wait_ge(y_done, h - 1)
                        pe.wait_ge(o_lo, 8 * T - 1)
                    elif G == 0:
                        pe.wait_ge(o_lo, 8 * T)
                    for f in fs:
                        last = three(nc, O(n), [oT[1 - tp][x][:, f, P * m:P * (m + 1)] for x in (0, 1)],
                                     [wo[x][:, f, HALF * n:HALF * (n + 1)] for x in (0, 1)], f == 0, f == KT - 1)
                    if fs[-1] == KT - 1:
                        last.then_inc(o_done, 1)

                def slot(t, par, g):
                    u = 8 * t + g
                    T, tp, G, proj = projected(t, par, g)
                    if attends(t, g, 2):
                        pe.wait_ge(probs, u - 1)
                        if after(t, g, 3):
                            pe.wait_ge(pt_lo, u - 2)
                        for c in range(2):
                            for m in range(TPB):
                                last = nc.tensor.transpose(
                                    TR[:, BLK * c + P * m:][:, :P],
                                    pr[g % 2][:, m, 2 * c:2 * c + 2, :].rearrange("p j s -> p (j s)"), ident[:])
                        last.then_inc(turned, 1)
                    if attends(t, g):
                        pe.wait_ge(q_lo, u + 1)
                        pe.wait_ge(k_loaded[g % 2], 16 * (4 * t + g // 2 + 1))
                        if after(t, g, 1):
                            pe.wait_ge(s_read, u)
                        for m in range(TPB):
                            last = three(nc, S[:, 256 * m:256 * (m + 1)],
                                         [qs[g % 2][x][:, P * m:P * (m + 1)] for x in (0, 1)],
                                         [kb[g % 2][:, x] for x in (0, 1)], True, True)
                        last.then_inc(scores, 1)
                    if proj:
                        if not looped(T) and T == 1 and G == 0:
                            pe.wait_ge(w_lo, KT)
                        output(T, tp, G, range(0, 4))
                    if attends(t, g, 2):
                        pe.wait_ge(pt_lo, u - 1)
                        pe.wait_ge(v_loaded[g % 2], 16 * (4 * t + g // 2))
                        if after(t, g, 3):
                            pe.wait_ge(o_lo, u - 2)
                        for c in range(2):
                            last = three(nc, V, [vb[g % 2][:, x, c] for x in (0, 1)],
                                         [pT[x][:, c] for x in (0, 1)], c == 0, c == 1)
                        last.then_inc(pv, 1)
                    if proj:
                        output(T, tp, G, range(4, KT))

                blocks(slot)(pe)

            @block.scalar
            def _(act):
                def split_q(t, g):
                    act.wait_ge(q_loaded[g % 2], 16 * (4 * t + g // 2 + 1))
                    if after(t, g, 2):
                        act.wait_ge(scores, 8 * t + g - 1)
                    nc.scalar.copy(qs[g % 2][0][:], qf[g % 2][:]).then_inc(q_hi, 1)

                split_q(0, 0)

                def slot(t, par, g):
                    u = 8 * t + g
                    T, _, G, _ = projected(t, par, g)
                    if attends(t, g, 2):
                        act.wait_ge(turned, u - 1)
                        if after(t, g, 3):
                            act.wait_ge(pv, u - 2)
                        nc.scalar.copy(pT[0][:].rearrange("p c n -> p (c n)"), TR).then_inc(pt_hi, 1)
                    if attends(t, g, -1):
                        split_q(t, g + 1)
                    n = lagging(T, G)
                    if n is not None:
                        act.wait_ge(coef, 4 * (n + 1))
                        yb = y[(G // 2 + 1) % 2]
                        nc.scalar.activation(yb[:], yb[:], ACT.Identity, scale=rstd[:], bias=nbias[:])\
                            .then_inc(applied, 1)
                    if attends(t, g):
                        act.wait_ge(centered, u + 1)
                        e = pr[g % 2][:].rearrange("p m j s -> p (m j s)")
                        nc.scalar.activation(e, e, ACT.Exp).then_inc(exped, 1)
                    if attends(t, g, 2):
                        act.wait_ge(pv, u - 1)
                        nc.scalar.copy(oT[par if g >= 2 else 1 - par][0][:, (g - 2) % KT], V).then_inc(o_hi, 1)
                    if not looped(t) and t == 0:
                        act.wait_ge(w_loaded[g % 2], 16 * (g // 2 + 1))
                        nc.scalar.copy(wo[0][:, g], y[g % 2][:]).then_inc(w_hi, 1)

                blocks(slot)(act)
                act.wait_ge(coef, 4 * NTILE)
                yb = y[(NTILE - 1) % 2]
                nc.scalar.activation(yb[:], yb[:], ACT.Identity, scale=rstd[:], bias=nbias[:]).then_inc(applied, 1)

            @block.vector
            def _(dve):
                def scale_by_gamma(n, yb):
                    dve.wait_ge(applied, n + 1)
                    nc.vector.tensor_tensor(yb[:], yb[:], gam[:], ALU.mult).then_inc(scaled, 1)

                def statistics_ready(n):
                    dve.wait_ge(st_done, 2 * (n + 1))
                    if looped(n) or n:
                        dve.wait_ge(coef, 4 * n)

                def slot(t, par, g):
                    u = 8 * t + g
                    T, _, G, proj = projected(t, par, g)
                    p = pr[g % 2]
                    heads = p[:].rearrange("p m j s -> p (m j) s")
                    n = lagging(T, G)
                    if n is not None and not attends(t, g):
                        statistics_ready(n)
                        nc.vector.bn_aggr(mv[:], st[:]).then_inc(aggr, 1)
                    if attends(t, g):
                        dve.wait_ge(scores, u + 1)
                        if g == 0:
                            dve.wait_ge(m_loaded, 16 * (t + 1))
                        if after(t, g, 2):
                            dve.wait_ge(turned, u - 1)
                        if n is not None:
                            statistics_ready(n)
                        for m in range(TPB):
                            last = nc.vector.scalar_tensor_tensor(
                                out=p[:, m], in0=S[:, 256 * m:256 * (m + 1)]
                                .rearrange("p (j s) -> p j s", j=GRP), scalar=SCALE0,
                                in1=mask[par][:, m, :].unsqueeze(1).to_broadcast([P, GRP, KEYS]),
                                op0=ALU.mult, op1=ALU.add)
                        last.then_inc(s_read, 1)
                        if n is not None:
                            nc.vector.bn_aggr(mv[:], st[:]).then_inc(aggr, 1)
                    if attends(t, g, 2):
                        dve.wait_ge(pt_hi, u - 1)
                        nc.vector.tensor_tensor(pT[1][:].rearrange("p c n -> p (c n)"), TR,
                                                f32(pT[0][:]).rearrange("p c n -> p (c n)"), ALU.subtract)\
                            .then_inc(pt_lo, 1)
                    if attends(t, g):
                        dve.wait_ge(s_read, u + 1)
                        if after(t, g, 1):
                            dve.wait_ge(centered, u)
                        nc.vector.tensor_reduce(mx[:], heads, AX_X, ALU.max).then_inc(maxed, 1)
                    if n is not None:
                        scale_by_gamma(n, y[(G // 2 + 1) % 2])
                    if attends(t, g):
                        dve.wait_ge(exped, u + 1)
                        nc.vector.tensor_reduce(sm[:], heads, AX_X, ALU.add).then_inc(summed, 1)
                        dve.wait_ge(summed, u + 1)
                        if after(t, g, 1):
                            dve.wait_ge(probs, u)
                        nc.vector.reciprocal(rs[:], sm[:]).then_inc(recips, 1)
                    if attends(t, g, 2):
                        dve.wait_ge(o_hi, u - 1)
                        o = oT[par if g >= 2 else 1 - par]
                        nc.vector.tensor_tensor(o[1][:, (g - 2) % KT], V, f32(o[0][:, (g - 2) % KT]), ALU.subtract)\
                            .then_inc(o_lo, 1)
                    if proj:
                        h = 8 * (T - 1) + G
                        m, half = divmod(G, 2)
                        cols = slice(HALF * half, HALF * (half + 1))
                        dve.wait_ge(o_done, h + 1)
                        dve.wait_ge(xbo, 4 * (T - 1) + m + 1)
                        if half == 0 and (looped(T) or 4 * (T - 1) + m >= 2):
                            dve.wait_ge(stored[m % 2], 16 * (2 * (T - 1) + m // 2))
                        nc.vector.tensor_tensor(y[m % 2][:, cols], O(half), xb[m % 2][:, cols], ALU.add)\
                            .then_inc(y_done, 1)
                        dve.wait_ge(y_done, h + 1)
                        nc.vector.bn_stats(st[:, half], y[m % 2][:, cols]).then_inc(st_done, 1)
                    if not looped(t) and t == 0:
                        dve.wait_ge(w_hi, g + 1)
                        nc.vector.tensor_tensor(wo[1][:, g], y[g % 2][:], f32(wo[0][:, g]), ALU.subtract)\
                            .then_inc(w_lo, 1)
                        if g == 3:
                            dve.wait_ge(c_loaded, 48)

                blocks(slot)(dve)
                statistics_ready(NTILE - 1)
                nc.vector.bn_aggr(mv[:], st[:]).then_inc(aggr, 1)
                scale_by_gamma(NTILE - 1, y[(NTILE - 1) % 2])

            @block.gpsimd
            def _(pool):
                nc.gpsimd.memset(mhalf[:], -0.5).then_inc(half_set, 1)
                nc.gpsimd.memset(eps[:], EPS0).then_inc(half_set, 1)
                nc.gpsimd.memset(minus[:], -1.0).then_inc(half_set, 1)
                pool.wait_ge(half_set, 3)

                def split_q(u, g):
                    pool.wait_ge(q_hi, u + 1)
                    nc.gpsimd.tensor_tensor(qs[g % 2][1][:], qf[g % 2][:], f32(qs[g % 2][0][:]), ALU.subtract)\
                        .then_inc(q_lo, 1)

                def coefficients(n):
                    pool.wait_ge(aggr, n + 1)
                    if looped(n) or n >= 1:
                        pool.wait_ge(applied, n)
                    nc.gpsimd.tensor_tensor(rstd[:], mv[:, 1:2], eps[:], ALU.add).then_inc(coef, 1)
                    nc.gpsimd.tensor_tensor(nbias[:], mv[:, 0:1], minus[:], ALU.mult).then_inc(coef, 1)
                    pool.wait_ge(coef, 4 * n + 2)
                    nc.gpsimd.tensor_tensor(rstd[:], rstd[:], mhalf[:], ALU.pow).then_inc(coef, 1)
                    pool.wait_ge(coef, 4 * n + 3)
                    nc.gpsimd.tensor_tensor(nbias[:], nbias[:], rstd[:], ALU.mult).then_inc(coef, 1)

                def shift_by_beta(n, yb):
                    pool.wait_ge(scaled, n + 1)
                    nc.gpsimd.tensor_tensor(yb[:], yb[:], bet[:], ALU.add).then_inc(normed, 1)

                split_q(0, 0)

                def slot(t, par, g):
                    u = 8 * t + g
                    T, _, G, _ = projected(t, par, g)
                    heads = pr[g % 2][:].rearrange("p m j s -> p (m j) s")
                    if attends(t, g, -1):
                        split_q(u + 1, g + 1)
                    n = lagging(T, G)
                    if n is not None:
                        coefficients(n)
                    if attends(t, g):
                        pool.wait_ge(maxed, u + 1)
                        nc.gpsimd.tensor_tensor(heads, heads, mx[:].unsqueeze(2).to_broadcast([P, TPB * GRP, KEYS]),
                                                ALU.subtract).then_inc(centered, 1)
                    if n is not None:
                        shift_by_beta(n, y[(G // 2 + 1) % 2])
                    if G % 2 == 1 and upcoming(T, G) is not None:
                        pool.wait_ge(x_loaded[(G // 2 + 1) % 2], 16 * (2 * (T - 1) + (G // 2 + 1) // 2 + 1))
                        if not looped(T) and T == 0:
                            pool.wait_ge(c_loaded, 48)
                        xr = xb[(G // 2 + 1) % 2]
                        nc.gpsimd.tensor_tensor(xr[:], xr[:], bo[:], ALU.add).then_inc(xbo, 1)
                    if attends(t, g):
                        pool.wait_ge(recips, u + 1)
                        nc.gpsimd.tensor_tensor(heads, heads, rs[:].unsqueeze(2).to_broadcast([P, TPB * GRP, KEYS]),
                                                ALU.mult).then_inc(probs, 1)

                blocks(slot)(pool)
                coefficients(NTILE - 1)
                shift_by_beta(NTILE - 1, y[(NTILE - 1) % 2])


def layer1(nc, ps, ident, x2_d, kmask_d, gate_d, a_d, b_d, out_d):
    M = SEQ // P
    with ExitStack() as mem:
        def sb(name, shape, dt=F32):
            return mem.enter_context(nc.sbuf_tensor(name, shape, dt))

        def sem(name):
            return mem.enter_context(nc.semaphore("b_" + name))

        A = [sb(f"A{x}", [P, KT, D], F32R) for x in "hl"]
        B = [sb(f"B{x}", [P, KT, D], F32R) for x in "hl"]
        raw2 = [sb(f"raw{i}", [P, 2, D]) for i in range(4)]
        raw = [raw2[k // 2][:, k % 2] for k in range(KT)]
        xt = [sb(f"x2t{i}", [P, D]) for i in range(4)]
        xT = [sb(f"x2T{x}", [P, KT, P], F32R) for x in "hl"]
        pr = sb("prob", [P, H1, KEYS])
        pT = [sb(f"probT{x}", [P, KT, P], F32R) for x in "hl"]
        km = sb("km", [P, BATCH, KEYS], U8)
        bias = sb("bias", [P, BATCH, KEYS])
        zero = sb("zero", [P, BATCH, KEYS])
        gate, gt = sb("gate", [P, 1]), sb("gt", [P, 1])
        mx, sm, rs = sb("mx1", [P, H1]), sb("sm1", [P, H1]), sb("rs1", [P, H1])

        (c_loaded, set_, masked, gated, a_hi, a_loe, a_loo, b_hi, b_loe, b_loo, a_free, b_free, x_turned, x_hi, x_lo,
         scores, s_read, maxed, centered, exped, summed, recips, probs, p_turned, p_hi, p_lo, o_done,
         out_done) = (sem(n) for n in (
             "c_loaded set masked gated a_hi a_loe a_loo b_hi b_loe b_loo a_free b_free x_turned x_hi x_lo scores "
             "s_read maxed centered exped summed recips probs p_turned p_hi p_lo o_done out_done").split())
        ab_loaded = [sem(f"ab_loaded{i}") for i in range(4)]
        x_loaded = [sem(f"x_loaded{i}") for i in range(4)]
        stored = [sem(f"stored{i}") for i in range(4)]
        S, XT, PT = ps[:, 0:1024], ps[:, 1024:2048], ps[:, 2048:3072]

        def O(n):
            return ps[:, 3072 + HALF * n:][:, :HALF]

        def batches(eng, slot):
            slot(0, 0, False)
            with eng.Fori(0, BATCH - 1) as b:
                for m in range(1, M):
                    slot(b, m, False)
                slot(b + 1, 0, False)
            for m in range(1, M):
                slot(BATCH - 1, m, True)

        def after(b, m, n):
            return not isinstance(b, int) or M * b + m >= n

        def hi(act, dst, c, b, first):
            k = c % KT
            act.wait_ge(ab_loaded[k // 2], 16 * (2 * b + c // KT + 1))
            if not first:
                if k < KT - 1:
                    act.wait_ge(a_free if c < KT else b_free, (KT - 1) * (b - 1) + k + 1)
                elif c < KT:
                    act.wait_ge(scores, M * b)
                else:
                    act.wait_ge(o_done, 2 * M * b)
            nc.scalar.copy(dst[0][:, k], raw[k]).then_inc(a_hi if c < KT else b_hi, 1)

        def lo(eng, sub, dst, c, b):
            k = c % KT
            eng.wait_ge(a_hi if c < KT else b_hi, KT * b + k + 1)
            done = (a_loo if k % 2 else a_loe) if c < KT else (b_loo if k % 2 else b_loe)
            sub(dst[1][:, k], raw[k], f32(dst[0][:, k]), ALU.subtract).then_inc(done, 1)

        with nc.Block() as block:
            @block.sync
            def _(sp):
                def load_x(u, i):
                    sp.dma_start(xt[i][:], x2_d[bass.ds(P * u, P), :]).then_inc(x_loaded[i], 16)

                def load_ab(b, c, first):
                    k = c % KT
                    if not first:
                        before = b if c >= KT else b - 1
                        for done in (a_loe, a_loo) if c >= KT else (b_loe, b_loo):
                            sp.wait_ge(done, KT // 2 * before + k // 2 + 1)
                    src = a_d if c < KT else b_d
                    sp.dma_start(raw2[k // 2][:], src[b][P * k:P * (k + 2), :].rearrange("(k p) n -> p k n", p=P))\
                        .then_inc(ab_loaded[k // 2], 16)

                load_x(0, 0)
                sp.dma_start(km[:], kmask_d.rearrange("b s -> (b s)").rearrange("(o n) -> o n", o=1)
                             .to_broadcast([P, BATCH * KEYS])).then_inc(c_loaded, 16)
                sp.dma_start(gate[:], gate_d.rearrange("(o n) -> o n", o=1).to_broadcast([P, 1])).then_inc(c_loaded, 16)
                for c in range(0, KT, 2):
                    load_ab(0, c, True)
                for i in range(1, 4):
                    load_x(i, i)
                for c in range(KT, 2 * KT, 2):
                    load_ab(0, c, False)

                def slot(b, m, last):
                    u = M * b + m
                    if m == 2 and not last:
                        for c in range(0, KT, 2):
                            load_ab(b + 1, c, False)
                    if m == 0 and (not isinstance(b, int) or b):
                        for c in range(KT, 2 * KT, 2):
                            load_ab(b, c, False)
                    if after(b, m, 1):
                        sp.wait_ge(out_done, 2 * u)
                        sp.dma_start(out_d[bass.ds(P * (u - 1), P), :], xt[(m - 1) % 4][:])\
                            .then_inc(stored[(m - 1) % 4], 16)
                        if not (last and m >= M - 3):
                            sp.wait_ge(stored[(m - 1) % 4], 16 * (2 * b + (m - 1) // 4 + 1))
                            load_x(u + 3, (m + 3) % 4)

                batches(sp, slot)
                sp.wait_ge(out_done, 2 * NTILE)
                sp.dma_start(out_d[P * (NTILE - 1):P * NTILE, :], xt[(NTILE - 1) % 4][:])\
                    .then_inc(stored[(NTILE - 1) % 4], 16)
                for i in range(4):
                    sp.wait_ge(stored[i], 16 * NTILE // 4)

            @block.tensor
            def _(pe):
                def turn_x(b, m):
                    u, i = M * b + m, m % 4
                    pe.wait_ge(x_loaded[i], 16 * (2 * b + m // 4 + 1))
                    if after(b, m, 1):
                        pe.wait_ge(x_lo, u)
                    for k in range(KT):
                        last = nc.tensor.transpose(XT[:, P * k:P * (k + 1)], xt[i][:, P * k:P * (k + 1)], ident[:])
                    last.then_inc(x_turned, 1)

                def output(u, b, m):
                    pe.wait_ge(p_lo, u + 1)
                    if not isinstance(u, int) or u >= 1:
                        pe.wait_ge(out_done, 2 * u)
                    for k in range(KT):
                        if m == 0:
                            pe.wait_ge(b_loo if k % 2 else b_loe, KT // 2 * b + k // 2 + 1)
                        for n in range(2):
                            last = three(nc, O(n), [pT[x][:, k] for x in (0, 1)],
                                         [B[x][:, k, HALF * n:HALF * (n + 1)] for x in (0, 1)], k == 0, k == KT - 1)
                            if k == KT - 1:
                                last.then_inc(o_done, 1)
                        if m == M - 1 and k < KT - 1:
                            last.then_inc(b_free, 1)

                def slot(b, m, last_batch):
                    u = M * b + m
                    pe.wait_ge(x_lo, u + 1)
                    if after(b, m, 1):
                        pe.wait_ge(s_read, u)
                    for k in range(KT):
                        if m == 0:
                            pe.wait_ge(a_loo if k % 2 else a_loe, KT // 2 * b + k // 2 + 1)
                        for n in range(2):
                            last = three(nc, S[:, HALF * n:HALF * (n + 1)], [xT[x][:, k] for x in (0, 1)],
                                         [A[x][:, k, HALF * n:HALF * (n + 1)] for x in (0, 1)], k == 0, k == KT - 1)
                        if m == M - 1 and k < KT - 1:
                            last.then_inc(a_free, 1)
                    last.then_inc(scores, 1)
                    if not (last_batch and m == M - 1):
                        turn_x(b, m + 1)
                    if after(b, m, 1):
                        if m:
                            output(u - 1, b, m - 1)
                        else:
                            output(u - 1, b - 1, M - 1)
                    pe.wait_ge(probs, u + 1)
                    if after(b, m, 1):
                        pe.wait_ge(p_lo, u)
                    for k in range(KT):
                        last = nc.tensor.transpose(PT[:, P * k:P * (k + 1)],
                                                   pr[:, 2 * k:2 * k + 2, :].rearrange("p h s -> p (h s)"), ident[:])
                    last.then_inc(p_turned, 1)

                turn_x(0, 0)
                batches(pe, slot)
                output(NTILE - 1, BATCH - 1, M - 1)

            @block.scalar
            def _(act):
                def split_x(u):
                    act.wait_ge(x_turned, u + 1)
                    nc.scalar.copy(xT[0][:].rearrange("p k c -> p (k c)"), XT).then_inc(x_hi, 1)

                act.wait_ge(c_loaded, 32)
                nc.scalar.activation(gt[:], gate[:], ACT.Tanh).then_inc(gated, 1)
                split_x(0)
                for c in range(KT):
                    hi(act, A, c, 0, True)

                def slot(b, m, last):
                    u = M * b + m
                    if not (last and m == M - 1):
                        if m == M - 1:
                            for c in range(3):
                                hi(act, A, c, b + 1, False)
                        split_x(u + 1)
                    act.wait_ge(centered, u + 1)
                    e = pr[:].rearrange("p h s -> p (h s)")
                    nc.scalar.activation(e, e, ACT.Exp).then_inc(exped, 1)
                    if m == M - 1 and not last:
                        for c in range(3, KT):
                            hi(act, A, c, b + 1, False)
                    act.wait_ge(p_turned, u + 1)
                    if after(b, m, 1):
                        act.wait_ge(o_done, 2 * u)
                    nc.scalar.copy(pT[0][:].rearrange("p k c -> p (k c)"), PT).then_inc(p_hi, 1)
                    if m == 0:
                        for c in range(KT, 2 * KT):
                            hi(act, B, c, b, isinstance(b, int))

                batches(act, slot)

            @block.vector
            def _(dve):
                nc.vector.memset(bias[:], float("-inf")).then_inc(set_, 1)
                nc.vector.memset(zero[:], 0.0).then_inc(set_, 1)
                dve.wait_ge(set_, 2)
                dve.wait_ge(c_loaded, 32)
                nc.vector.copy_predicated(bias[:], km[:], zero[:]).then_inc(masked, 1)
                dve.wait_ge(masked, 1)
                dve.wait_ge(gated, 1)

                def split_x(u):
                    dve.wait_ge(x_hi, u + 1)
                    nc.vector.tensor_tensor(xT[1][:].rearrange("p k c -> p (k c)"), XT,
                                            f32(xT[0][:]).rearrange("p k c -> p (k c)"), ALU.subtract)\
                        .then_inc(x_lo, 1)

                def finish(u, i):
                    for n in range(2):
                        dve.wait_ge(o_done, 2 * u + n + 1)
                        cols = slice(HALF * n, HALF * (n + 1))
                        nc.vector.scalar_tensor_tensor(out=xt[i][:, cols], in0=O(n), scalar=gt[:], in1=xt[i][:, cols],
                                                       op0=ALU.mult, op1=ALU.add).then_inc(out_done, 1)

                split_x(0)
                for c in range(1, KT, 2):
                    lo(dve, nc.vector.tensor_tensor, A, c, 0)

                def slot(b, m, last):
                    u = M * b + m
                    dve.wait_ge(scores, u + 1)
                    if after(b, m, 1):
                        dve.wait_ge(p_turned, u)
                    nc.vector.scalar_tensor_tensor(out=pr[:], in0=S.rearrange("p (h s) -> p h s", h=H1), scalar=SCALE1,
                                                   in1=bias[:, bass.ds(b, 1), :].to_broadcast([P, H1, KEYS]),
                                                   op0=ALU.mult, op1=ALU.add).then_inc(s_read, 1)
                    dve.wait_ge(s_read, u + 1)
                    nc.vector.tensor_reduce(mx[:], pr[:], AX_X, ALU.max).then_inc(maxed, 1)
                    if not (last and m == M - 1):
                        split_x(u + 1)
                        if m == M - 1:
                            lo(dve, nc.vector.tensor_tensor, A, 1, b + 1)
                    dve.wait_ge(exped, u + 1)
                    nc.vector.tensor_reduce(sm[:], pr[:], AX_X, ALU.add).then_inc(summed, 1)
                    dve.wait_ge(summed, u + 1)
                    nc.vector.reciprocal(rs[:], sm[:]).then_inc(recips, 1)
                    if m == M - 1 and not last:
                        for c in range(3, KT, 2):
                            lo(dve, nc.vector.tensor_tensor, A, c, b + 1)
                    if after(b, m, 1):
                        finish(u - 1, (m - 1) % 4)
                    dve.wait_ge(p_hi, u + 1)
                    nc.vector.tensor_tensor(pT[1][:].rearrange("p k c -> p (k c)"), PT,
                                            f32(pT[0][:]).rearrange("p k c -> p (k c)"), ALU.subtract)\
                        .then_inc(p_lo, 1)
                    if m == 0:
                        for c in range(KT + 1, 2 * KT, 2):
                            lo(dve, nc.vector.tensor_tensor, B, c, b)

                batches(dve, slot)
                finish(NTILE - 1, (NTILE - 1) % 4)

            @block.gpsimd
            def _(pool):
                for c in range(0, KT, 2):
                    lo(pool, nc.gpsimd.tensor_tensor, A, c, 0)

                def slot(b, m, last):
                    u = M * b + m
                    pool.wait_ge(maxed, u + 1)
                    nc.gpsimd.tensor_tensor(pr[:], pr[:], mx[:].unsqueeze(2).to_broadcast([P, H1, KEYS]),
                                            ALU.subtract).then_inc(centered, 1)
                    if m == M - 1 and not last:
                        for c in (0, 2):
                            lo(pool, nc.gpsimd.tensor_tensor, A, c, b + 1)
                    pool.wait_ge(recips, u + 1)
                    nc.gpsimd.tensor_tensor(pr[:], pr[:], rs[:].unsqueeze(2).to_broadcast([P, H1, KEYS]),
                                            ALU.mult).then_inc(probs, 1)
                    if m == M - 1 and not last:
                        for c in (4, 6):
                            lo(pool, nc.gpsimd.tensor_tensor, A, c, b + 1)
                    if m == 0:
                        for c in range(KT, 2 * KT, 2):
                            lo(pool, nc.gpsimd.tensor_tensor, B, c, b)

                batches(pool, slot)


def build(nc, i, out):
    q_d = nc.dram_tensor("q_scratch", [NBLK, KT, P, BLK], F32).ap()
    x2_d = nc.dram_tensor("x2_scratch", [TOKENS, D], F32).ap()
    kbd_d = nc.dram_tensor("kbd_scratch", [BATCH, KVH0, P, 2 * GRP * KEYS], F32).ap()
    vbd_d = nc.dram_tensor("vbd_scratch", [BATCH, KVH0, P, 4 * P], F32).ap()
    a_d = nc.dram_tensor("a_scratch", [BATCH, D, D], F32).ap()
    b_d = nc.dram_tensor("b_scratch", [BATCH, D, D], F32).ap()
    x_d = i["x"].rearrange("b s d -> (b s) d")
    ctx_d = i["ctx_2048"].rearrange("b s d -> (b s) d")
    mask_d = i["mask_Bx1xSxS2_ff0"].rearrange("b o s k -> (b o s) k")
    w = {"Wk1": i["L1_xattn_Wk"], "Wv1": i["L1_xattn_Wv"], "Wq1": i["L1_xattn_Wq"], "Wo1": i["L1_xattn_Wo"],
         "gamma1": i["L1_xattn_ln_gamma"], "beta1": i["L1_xattn_ln_beta"]}
    for n in ("Wq", "Wk", "Wv", "Wo", "bq", "bk", "bv", "bo", "gamma", "beta"):
        w[n + "0"] = i["L0_xattn_" + n]
    with ExitStack() as mem:
        ident = mem.enter_context(nc.sbuf_tensor("ident", [P, P], F32))
        ps = mem.enter_context(nc.psum_tensor("ps", [P, 8 * HALF], F32))
        with ExitStack() as tables:
            normT = [tables.enter_context(nc.sbuf_tensor(f"normT{x}", [P, KT, CTX], F32R)) for x in "hl"]
            context_tables(nc, ps, ident, normT, ctx_d, w, kbd_d, vbd_d)
            layer1_tables(nc, ps, ident, normT, w, a_d, b_d)
        q_projection(nc, ps, ident, x_d, w, q_d)
        layer0(nc, ps, ident, x_d, q_d, mask_d, kbd_d, vbd_d, w, x2_d)
        layer1(nc, ps, ident, x2_d, i["mask_BxS2_bf1"], i["L1_xattn_gate"], a_d, b_d,
               out.rearrange("b s d -> (b s) d"))


_INS = ['x', 'ctx_2048', 'mask_Bx1xSxS2_ff0', 'mask_BxS2_bf1', 'L0_xattn_Wq', 'L0_xattn_bq', 'L0_xattn_Wk',
        'L0_xattn_bk', 'L0_xattn_Wv', 'L0_xattn_bv', 'L0_xattn_Wo', 'L0_xattn_bo', 'L0_xattn_gamma', 'L0_xattn_beta',
        'L1_xattn_Wq', 'L1_xattn_Wk', 'L1_xattn_Wv', 'L1_xattn_Wo', 'L1_xattn_ln_gamma', 'L1_xattn_ln_beta',
        'L1_xattn_gate']


def kernel(**inputs):
    import numpy as _np
    import concourse.bacc as _bacc
    from concourse import mybir as _mybir
    from concourse.bass_utils import run_bass_kernel_spmd as _run

    nc = _bacc.Bacc("TRN2", target_bir_lowering=False, num_devices=1)
    arrays, args = {}, {}
    for name in _INS:
        a = _np.ascontiguousarray(inputs[name])
        arrays[f"in_{name}_dram"] = a
        args[name] = nc.dram_tensor(f"in_{name}_dram", a.shape, _mybir.dt.from_np(a.dtype), kind="ExternalInput").ap()
    out = nc.dram_tensor("out_0_dram", (BATCH, SEQ, D), F32, kind="ExternalOutput").ap()
    build(nc, args, out)
    r = _run(nc, [arrays], core_ids=[0])
    return r.results[0]["out_0_dram"]
```
